# Optimizing a Trainium2 kernel written in Bass

```python
import numpy as np
import jax
import jax.numpy as jnp

def _softmax(x, axis=-1):
    return jax.nn.softmax(x, axis=axis)

def _gelu(x):
    return jax.nn.gelu(x, approximate=True)

def _silu(x):
    return jax.nn.silu(x)

def _sigmoid(x):
    return jax.nn.sigmoid(x)

def _layernorm(x, axis=-1, eps=1e-05):
    m = jnp.mean(x, axis=axis, keepdims=True)
    v = jnp.var(x, axis=axis, keepdims=True)
    return (x - m) / jnp.sqrt(v + eps)

def _scatter_add(tgt, idx, src, axis=0):
    return tgt.at[idx].add(src)

def _segment_sum(src, seg, n):
    return jax.ops.segment_sum(src, seg, n)
kernel_name = 'mk_xattn_seq_d1_seqx_r4_71cd49'

def setup_inputs(seed: int=0):
    np.random.seed(seed)
    _w = jnp.asarray

    def _rec_inputs():
        import jax
        import jax.numpy as jnp
        _rk = jax.random.key(seed)
        x = -0.000125 + 0.9999 * jax.random.normal(jax.random.fold_in(_rk, 1), (16, 112, 512), jnp.float32)
        _lenS = 112 - jax.random.randint(jax.random.fold_in(_rk, 7), (16,), 0, max(1, 112 // 4) + 1, jnp.int32)
        _lenS2 = 375 - jax.random.randint(jax.random.fold_in(_rk, 8), (16,), 0, max(1, 375 // 4) + 1, jnp.int32)
        _ctx_1024P = jax.random.normal(jax.random.fold_in(_rk, 11), (16, 16, 256), jnp.float32)
        _ctx_1024c = jax.random.dirichlet(jax.random.fold_in(_rk, 511), 0.3 * jnp.ones((16,), jnp.float32), (16, 375))
        _ctx_1024t = jnp.einsum('bsk,bkd->bsd', _ctx_1024c, _ctx_1024P)
        _ctx_1024t = _ctx_1024t * jax.lax.rsqrt(jnp.mean(jnp.square(_ctx_1024t)) + 1e-12) * 0.953939
        ctx_1024 = 4.13588e-05 + 0.999923 * (_ctx_1024t + 0.3 * jax.random.normal(jax.random.fold_in(_rk, 611), (16, 375, 256), jnp.float32))
        return (x, ctx_1024)
    x, ctx_1024 = _rec_inputs()

    def _L0_xattn_setup():
        import jax, jax.numpy as jnp
        import numpy as np
        EPS = 1e-06

        def _rmsnorm(x, w):
            var = jnp.mean(jnp.square(x), axis=-1, keepdims=True)
            return x * jax.lax.rsqrt(var + EPS) * w
        key = jax.random.key(seed)
        ks = jax.random.split(key, 6)
        B, N, M = (4, 1024, 512)
        d_model, memory_dim = (512, 256)
        hidden_states = jax.random.normal(ks[0], (B, N, d_model), dtype=jnp.float32)
        memory = jax.random.normal(ks[1], (B, M, memory_dim), dtype=jnp.float32)
        W_mem = jax.random.normal(ks[2], (d_model, memory_dim), dtype=jnp.float32) / np.sqrt(memory_dim)
        W_gate = jax.random.normal(ks[3], (d_model, 2 * d_model), dtype=jnp.float32) / np.sqrt(2 * d_model)
        b_gate = jax.random.normal(ks[4], (d_model,), dtype=jnp.float32) * 0.01
        norm_w = jnp.ones((d_model,), dtype=jnp.float32)
        return {'hidden_states': hidden_states, 'memory': memory, 'W_mem': W_mem, 'W_gate': W_gate, 'b_gate': b_gate, 'norm_w': norm_w}
    _L0_xattn_all = _L0_xattn_setup()
    _L0_xattn_in = {k: v for k, v in _L0_xattn_all.items() if k in ('W_mem', 'W_gate', 'b_gate', 'norm_w')}
    del _L0_xattn_all
    return {'x': x, 'ctx_1024': ctx_1024, 'L0_xattn_W_mem': _L0_xattn_in['W_mem'], 'L0_xattn_W_gate': _L0_xattn_in['W_gate'], 'L0_xattn_b_gate': _L0_xattn_in['b_gate'], 'L0_xattn_norm_w': _L0_xattn_in['norm_w']}

def reference(x, ctx_1024, L0_xattn_W_mem, L0_xattn_W_gate, L0_xattn_b_gate, L0_xattn_norm_w):
    import jax
    import jax.numpy as jnp

    def _L0_xattn_ref(hidden_states, memory, W_mem, W_gate, b_gate, norm_w):
        import jax, jax.numpy as jnp
        import numpy as np
        EPS = 1e-06

        def _rmsnorm(x, w):
            var = jnp.mean(jnp.square(x), axis=-1, keepdims=True)
            return x * jax.lax.rsqrt(var + EPS) * w
        D = hidden_states.shape[-1]
        memory_proj = jnp.einsum('bme,de->bmd', memory, W_mem)
        scores = jnp.einsum('bnd,bmd->bnm', hidden_states, memory_proj) / jnp.sqrt(jnp.float32(D))
        attn = jax.nn.softmax(scores, axis=-1)
        memory_context = jnp.einsum('bnm,bmd->bnd', attn, memory_proj)
        gate_input = jnp.concatenate([hidden_states, memory_context], axis=-1)
        gate = jax.nn.sigmoid(jnp.einsum('bnf,df->bnd', gate_input, W_gate) + b_gate)
        fused = hidden_states + gate * memory_context
        return _rmsnorm(fused, norm_w)
    x = _L0_xattn_ref(x, ctx_1024, L0_xattn_W_mem, L0_xattn_W_gate, L0_xattn_b_gate, L0_xattn_norm_w)
    return x

_drawn_inputs = setup_inputs


def setup_inputs(seed=0):
    import zlib

    import numpy as np

    out = dict(_drawn_inputs(seed))
    spreads = {'L0_xattn_norm_w': (1.0, 0.2)}
    factors = {'L0_xattn_b_gate': 50.776}
    for name, (base, spread) in spreads.items():
        noise = np.random.default_rng([zlib.crc32(name.encode()), seed]).standard_normal(out[name].shape)
        drawn = base * np.exp(spread * noise) if base else spread * noise
        out[name] = jnp.asarray(drawn.astype(out[name].dtype))
    for name, factor in factors.items():
        out[name] = (out[name] * factor).astype(out[name].dtype)
    return out
```

```python
from contextlib import ExitStack

import concourse.bass as bass
from concourse import mybir

ALU = mybir.AluOpType
ACT = mybir.ActivationFunctionType
AX = mybir.AxisListType
F32 = mybir.dt.float32
F32R = mybir.dt.float32r

P = 128
B, N, M, D, E = 16, 112, 375, 512, 256
GROUP = 4
G = B // GROUP
NG = GROUP * N
KD, KE = D // P, E // P
MT = -(-M // P)
MROWS = [min(P, M - P * t) for t in range(MT)]
SCORE_SCALE = float(D) ** -0.5
EPS = 1e-6
WARM_UP = 8
DVE_OUT = KD - 1
HALVES = [slice(0, NG // 2), slice(NG // 2, NG)]
ALL = slice(0, NG)


def build(nc: bass.Bass, xT, memT, memN, w_mem, w_memT, w_gateT, vecs, outT):
    with ExitStack() as ctx:
        def sb(name, shape, dt=F32):
            return ctx.enter_context(nc.sbuf_tensor(name, shape, dt))

        def bank(name):
            return ctx.enter_context(nc.psum_tensor(name, [P, 512], F32))

        def sem(name):
            return ctx.enter_context(nc.semaphore(name))

        x = sb("x", [P, G, KD, NG])
        x_hi = sb("x_hi", [P, G, KD, NG], F32R)
        x_lo = sb("x_lo", [P, G, KD, NG], F32R)
        wq = sb("wq", [P, KD, E])
        wq_hi = sb("wq_hi", [P, KD, E], F32R)
        wq_lo = sb("wq_lo", [P, KD, E], F32R)
        wc = sb("wc", [P, KE, D])
        wc_hi = sb("wc_hi", [P, KE, D], F32R)
        wc_lo = sb("wc_lo", [P, KE, D], F32R)
        wg = sb("wg", [P, 2 * KD, D])
        wg_hi = sb("wg_hi", [P, KD, D], F32R)
        wg_lo = sb("wg_lo", [P, KD, D], F32R)
        ww_hi = sb("ww_hi", [P, KE, D], F32R)
        ww_lo = sb("ww_lo", [P, KE, D], F32R)
        bw = sb("bw", [P, 2 * KD])
        half_b = sb("half_b", [P, KD])
        ident = sb("ident", [N, N])
        mean_of = sb("mean_of", [P, P])
        mem_t = sb("mem_t", [P, GROUP, KE * M])
        mem_n = sb("mem_n", [P, GROUP, MT * E])
        qT = sb("qT", [P, KE, NG])
        neg_max = sb("neg_max", [P, GROUP])
        row_sum = sb("row_sum", [P, GROUP])
        row_inv = sb("row_inv", [P, GROUP])
        probs = sb("probs", [P, GROUP, M])
        probsT = sb("probsT", [P, 2, MT * N])
        aT_hi = sb("aT_hi", [P, 2, KE, NG], F32R)
        aT_lo = sb("aT_lo", [P, 2, KE, NG], F32R)
        spent = wg[:, KD:].rearrange("p k d -> p (k d)")
        gated = spent[:, 0:2 * NG].rearrange("p (s n) -> p s n", s=2)
        squares = spent[:, 2 * NG:4 * NG].rearrange("p (s n) -> p s n", s=2)
        sq_sum = sb("sq_sum", [P, NG])
        rstd = sb("rstd", [P, NG])
        eps = sb("eps", [P, 1])

        p_scores = bank("p_scores")
        p_probsT = bank("p_probsT")
        p_aT = bank("p_aT")
        p_q0 = bank("p_q0")
        p_logit = [bank("p_logit0"), bank("p_logit1")]
        p_ctx = [bank("p_ctx0"), bank("p_ctx1")]
        p_q = [p_q0, p_aT]
        p_scores_first = [p_scores, p_ctx[0], p_ctx[1], p_logit[1]]
        p_ww = [p_logit[0], p_q0]
        p_probsT_first = [p_probsT, p_scores, p_ctx[0], p_ctx[1]]

        ld_x = [sem(f"ld_x_{g}") for g in range(G)]
        ld_x0 = [sem(f"ld_x0_{k}") for k in range(KD)]
        ld_wq = [sem(f"ld_wq_{k}") for k in range(KD)]
        ld_wc, ld_wg1, ld_wg2, ld_bw = (sem(n) for n in ("ld_wc", "ld_wg1", "ld_wg2", "ld_bw"))
        ld_memT = [sem(f"ld_memT{j}") for j in range(GROUP)]
        ld_memN = [sem(f"ld_memN{j}") for j in range(GROUP)]
        stored = sem("stored")
        zeroed, consts, bias_halved = sem("zeroed"), sem("consts"), sem("bias_halved")
        x0_hi, x0_lo, x1_hi, xs_hi, x1_lo, xs_lo = (sem(n) for n in ("x0_hi", "x0_lo", "x1_hi", "xs_hi", "x1_lo", "xs_lo"))
        wq_hi_ok, wq_lo_ok = sem("wq_hi_ok"), sem("wq_lo_ok")
        wc_hi_ok, wc_lo_ok = sem("wc_hi_ok"), sem("wc_lo_ok")
        wg_hi_ok, wg_lo_ok = sem("wg_hi_ok"), sem("wg_lo_ok")
        ww_made, ww_hi_ok, ww_lo_ok = sem("ww_made"), sem("ww_hi_ok"), sem("ww_lo_ok")
        q_made, q_ready = sem("q_made"), sem("q_ready")
        scores_made, max_made, exp_made, inv_made, probs_ready = (
            sem(n) for n in ("scores_made", "max_made", "exp_made", "inv_made", "probs_ready"))
        probsT_made, probsT_ready = sem("probsT_made"), sem("probsT_ready")
        aT_made, aT_hi_ready, aT_lo_ready = sem("aT_made"), sem("aT_hi_ready"), sem("aT_lo_ready")
        logit_made, ctx_made, tanh_made, gated_made, fused_made, sq_made = (
            sem(n) for n in ("logit_made", "ctx_made", "tanh_made", "gated_made", "fused_made", "sq_made"))
        sq_added, weighted = sem("sq_added"), sem("weighted")
        sq_sum_made, mean_made, log_made, rstd_made, out_made, pool_out_made = (
            sem(n) for n in ("sq_sum_made", "mean_made", "log_made", "rstd_made", "out_made", "pool_out_made"))

        def f32(ap):
            return ap.bitcast(F32)

        block = ctx.enter_context(nc.Block())

        @block.sync
        def _(sp):
            def load_memT(b, j):
                sp.dma_start(mem_t[:, j, :], memT[b]).then_inc(ld_memT[j], 16)

            def load_memN(b, j):
                sp.dma_start(mem_n[:, j, :], memN[b]).then_inc(ld_memN[j], 16)

            for k in range(KD):
                sp.dma_start(wq[:, k], w_mem[:, k]).then_inc(ld_wq[k], 16)
                sp.dma_start(x[:, 0, k], xT[0, :, k]).then_inc(ld_x0[k], 16)
            load_memT(0, 0)
            sp.dma_start(wg[:, KD:], w_gateT[:, KD:]).then_inc(ld_wg2, 16)
            for j in range(1, GROUP):
                load_memT(j, j)
            sp.dma_start(wg[:, 0:KD], w_gateT[:, 0:KD]).then_inc(ld_wg1, 16)
            for j in range(GROUP):
                load_memN(j, j)
            sp.dma_start(wc[:, :, :], w_memT).then_inc(ld_wc, 16)
            sp.dma_start(bw[:, :], vecs).then_inc(ld_bw, 16)
            for g in range(1, G):
                sp.dma_start(x[:, g], xT[g]).then_inc(ld_x[g], 16)
            with sp.Fori(1, G) as g:
                for j in range(GROUP):
                    sp.wait_ge(aT_made, GROUP * g + (j - GROUP + 1))
                    load_memT(GROUP * g + j, j)
                    load_memN(GROUP * g + j, j)
            with sp.Fori(0, G - 1) as g:
                for c in range(KD):
                    if c < DVE_OUT:
                        sp.wait_ge(out_made, DVE_OUT * g + c + 1)
                    else:
                        sp.wait_ge(pool_out_made, (KD - DVE_OUT) * g + c - DVE_OUT + 1)
                    sp.dma_start(outT[g, :, c], x[:, g, c]).then_inc(stored, 16)
            for h, rows in enumerate(HALVES):
                for c in range(KD):
                    if c < DVE_OUT:
                        sp.wait_ge(out_made, DVE_OUT * (G - 1 + h) + c + 1)
                    else:
                        sp.wait_ge(pool_out_made, (KD - DVE_OUT) * (G - 1 + h) + c - DVE_OUT + 1)
                    sp.dma_start(outT[G - 1, :, c, rows], x[:, G - 1, c, rows]).then_inc(stored, 16)
            sp.wait_ge(stored, 16 * KD * (G + 1))

        @block.tensor
        def _(pe):
            def three(out, w_hi, w_lo, m_hi, m_lo, first, last):
                pe.matmul(out, w_hi, m_hi, start=first, stop=False)
                pe.matmul(out, w_lo, m_hi, start=False, stop=False)
                return pe.matmul(out, w_hi, m_lo, start=False, stop=last)

            def q_part(g, e, k):
                return three(p_q[e][:, 0:NG], wq_hi[:, k, e * P:(e + 1) * P], wq_lo[:, k, e * P:(e + 1) * P],
                             x_hi[:, g, k], x_lo[:, g, k], k == 0, k == KD - 1)

            def product_of_weights(e):
                for k in range(KD):
                    mm = pe.matmul(p_ww[e][:, 0:D], wq[:, k, e * P:(e + 1) * P], wg[:, KD + k],
                                   start=(k == 0), stop=(k == KD - 1))
                mm.then_inc(ww_made, 1)

            def score(b, j, into=p_scores):
                pe.wait_ge(ld_memT[j], 16 * (b // GROUP + 1) if isinstance(b, int) else b * 4 + (16 - 4 * j))
                for e in range(KE):
                    mm = pe.matmul(into[0:N, 0:M], qT[:, e, j * N:(j + 1) * N],
                                   mem_t[:, j, e * M:(e + 1) * M], start=(e == 0), stop=(e == KE - 1))
                mm.then_inc(scores_made, 1)

            def transpose_probs(b, j, into=p_probsT):
                pe.wait_ge(probs_ready, b + 1)
                for t in range(MT):
                    mm = pe.transpose(into[0:MROWS[t], t * N:(t + 1) * N],
                                      probs[0:N, j, t * P:t * P + MROWS[t]], ident[:, :])
                mm.then_inc(probsT_made, 1)

            def attend(b, j):
                pe.wait_ge(probsT_ready, b + 1)
                pe.wait_ge(ld_memN[j], 16 * (b // GROUP + 1) if isinstance(b, int) else b * 4 + (16 - 4 * j))
                for e in range(KE):
                    for t in range(MT):
                        mm = pe.matmul(p_aT[:, e * N:(e + 1) * N],
                                       mem_n[0:MROWS[t], j, t * E + e * P:t * E + (e + 1) * P],
                                       probsT[0:MROWS[t], j % 2, t * N:(t + 1) * N],
                                       start=(t == 0), stop=(t == MT - 1))
                mm.then_inc(aT_made, 1)

            def logits_from_x(g, c, ks=range(KD)):
                for k in ks:
                    mm = three(p_logit[c % 2][:, 0:NG], wg_hi[:, k, c * P:(c + 1) * P],
                               wg_lo[:, k, c * P:(c + 1) * P], x_hi[:, g, k], x_lo[:, g, k], k == 0, False)
                return mm

            def logits_from_a(g, c, par):
                for e in range(KE):
                    mm = three(p_logit[c % 2][:, 0:NG], ww_hi[:, e, c * P:(c + 1) * P],
                               ww_lo[:, e, c * P:(c + 1) * P], aT_hi[:, par, e], aT_lo[:, par, e],
                               False, e == KE - 1)
                mm.then_inc(logit_made, 1)

            def context(g, c, par, into=None, rows=ALL):
                into = into or p_ctx[c % 2]
                for e in range(KE):
                    mm = three(into[:, rows], wc_hi[:, e, c * P:(c + 1) * P], wc_lo[:, e, c * P:(c + 1) * P],
                               aT_hi[:, par, e, rows], aT_lo[:, par, e, rows], e == 0, e == KE - 1)
                mm.then_inc(ctx_made, 1)

            def mean_square(count, into=p_logit[1], rows=ALL):
                pe.wait_ge(sq_sum_made, count)
                pe.matmul(into[:, rows], mean_of[:, :], sq_sum[:, rows], start=True, stop=True).then_inc(mean_made, 1)

            pe.wait_ge(consts, 1)
            for _ in range(WARM_UP):
                pe.matmul(p_scores[:, 0:P], mean_of[:, :], mean_of[:, :], start=True, stop=True)

            for k in range(KD):
                pe.wait_ge(wq_lo_ok, k + 1)
                pe.wait_ge(x0_lo, k + 1)
                for e in range(KE):
                    mm = q_part(0, e, k)
                    if k == KD - 1:
                        mm.then_inc(q_made, 1)
            pe.wait_ge(ld_wg2, 16)
            product_of_weights(0)
            pe.wait_ge(q_ready, KE)
            for j in range(GROUP):
                score(j, j, p_scores_first[j])
            product_of_weights(1)
            pe.wait_ge(consts, 2)
            pe.wait_ge(ww_lo_ok, 1)
            for j in range(GROUP + 1):
                if j < GROUP:
                    transpose_probs(j, j, p_probsT_first[j])
                    pe.wait_ge(wg_lo_ok, j + 1)
                    logits_from_x(0, 0, [j])
                if j:
                    if j > 1:
                        pe.wait_ge(aT_lo_ready, j - 1)
                    attend(j - 1, j - 1)
            pe.wait_ge(wc_lo_ok, KE)
            pe.wait_ge(ww_lo_ok, KE)

            with pe.Fori(1, G) as g:
                par = (g + 1) % 2
                pe.wait_ge(xs_lo, g)
                for e in range(KE):
                    if e:
                        pe.wait_ge(aT_lo_ready, GROUP * g)
                    for k in range(KD):
                        mm = q_part(g, e, k)
                    mm.then_inc(q_made, 1)
                for j in range(GROUP):
                    b = GROUP * g + j
                    if j == 0:
                        logits_from_a(g - 1, 0, par)
                        pe.wait_ge(q_ready, KE * g + KE)
                        score(b, j)
                        context(g - 1, 0, par)
                        logits_from_x(g - 1, 1, range(0, KD // 2))
                        transpose_probs(b, j)
                        logits_from_x(g - 1, 1, range(KD // 2, KD))
                    elif j < GROUP - 1:
                        pe.wait_ge(exp_made, b)
                        score(b, j)
                        logits_from_a(g - 1, j, par)
                        if j >= 2:
                            pe.wait_ge(gated_made, KD * g + (j - 1 - KD))
                        context(g - 1, j, par)
                        transpose_probs(b, j)
                        pe.wait_ge(tanh_made, KD * g + (j - KD))
                        logits_from_x(g - 1, j + 1)
                    else:
                        logits_from_a(g - 1, j, par)
                        pe.wait_ge(gated_made, KD * g + (j - 1 - KD))
                        context(g - 1, j, par)
                        pe.wait_ge(exp_made, b)
                        score(b, j)
                        pe.wait_ge(tanh_made, KD * g + (j - KD))
                        logits_from_x(g, 0)
                        transpose_probs(b, j)
                        mean_square(g)
                    pe.wait_ge(aT_lo_ready, b)
                    attend(b, j)

            par = (G - 1) % 2
            first = KD * (G - 1)
            pe.wait_ge(log_made, G - 1)
            logits_from_x(G - 1, 1)
            pe.wait_ge(aT_lo_ready, B)
            for c in range(KD):
                logits_from_a(G - 1, c, par)
                if c >= 2:
                    pe.wait_ge(gated_made, first + c - 1)
                if c < KD - 1:
                    context(G - 1, c, par)
                if 1 <= c < KD - 1:
                    pe.wait_ge(tanh_made, first + c)
                    logits_from_x(G - 1, c + 1)
            for h, rows in enumerate(HALVES):
                if h == 1:
                    pe.wait_ge(gated_made, first + KD - 1)
                context(G - 1, KD - 1, par, p_ctx[(KD - 1 + h) % 2], rows)
            for h, rows in enumerate(HALVES):
                mean_square(G + h, [p_logit[0], p_scores][h], rows)

        @block.scalar
        def _(act):
            def exponentials(b, j, scores=p_scores):
                act.wait_ge(max_made, b + 1)
                nc.scalar.activation(probs[0:N, j], scores[0:N, 0:M], ACT.Exp, bias=neg_max[0:N, j:j + 1],
                                     accum_out=row_sum[0:N, j:j + 1]).then_inc(exp_made, 1)

            def read_q(g):
                for e in range(KE):
                    act.wait_ge(q_made, KE * g + e + 1)
                    nc.scalar.activation(qT[:, e], p_q[e][:, 0:NG], ACT.Copy, scale=SCORE_SCALE).then_inc(q_ready, 1)

            def high_a(b, j, par):
                act.wait_ge(aT_made, b + 1)
                nc.scalar.activation(aT_hi[:, par, :, j * N:(j + 1) * N],
                                     p_aT[:, 0:KE * N].rearrange("p (e n) -> p e n", e=KE),
                                     ACT.Copy).then_inc(aT_hi_ready, 1)

            def tanh(g, c):
                act.wait_ge(logit_made, KD * g + c + 1)
                nc.scalar.activation(gated[:, c % 2], p_logit[c % 2][:, 0:NG], ACT.Tanh, bias=half_b[:, c:c + 1],
                                     scale=0.5).then_inc(tanh_made, 1)

            def square(g, c, h=0, rows=ALL):
                act.wait_ge(fused_made, KD * g + c + h + 1)
                if c >= 2:
                    act.wait_ge(sq_added, (KD - 2) * g + 1)
                nc.scalar.activation(squares[:, c % 2, rows], x[:, g, c, rows], ACT.Square).then_inc(sq_made, 1)

            def weight(g, c, h=0, rows=ALL):
                nc.scalar.activation(x[:, g, c, rows], x[:, g, c, rows], ACT.Copy,
                                     scale=bw[:, KD + c:KD + c + 1]).then_inc(weighted, 1)

            def root(count, mean=p_logit[1], rows=ALL):
                act.wait_ge(mean_made, count)
                nc.scalar.activation(rstd[:, rows], mean[:, rows], ACT.Ln, bias=eps[:, 0:1]).then_inc(log_made, 1)
                act.wait_ge(log_made, count)
                nc.scalar.activation(rstd[:, rows], rstd[:, rows], ACT.Exp, scale=-0.5).then_inc(rstd_made, 1)

            for k in range(KD):
                act.wait_ge(ld_wq[k], 16)
                nc.scalar.activation(wq_hi[:, k], wq[:, k], ACT.Copy).then_inc(wq_hi_ok, 1)
                act.wait_ge(ld_x0[k], 16)
                nc.scalar.activation(x_hi[:, 0, k], x[:, 0, k], ACT.Copy).then_inc(x0_hi, 1)
            read_q(0)

            def high_ww(e):
                act.wait_ge(ww_made, e + 1)
                nc.scalar.activation(ww_hi[:, e], p_ww[e][:, 0:D], ACT.Copy).then_inc(ww_hi_ok, 1)

            high_ww(0)
            for j in range(GROUP):
                exponentials(j, j, p_scores_first[j])
            act.wait_ge(ld_wg1, 16)
            for k in range(KD):
                nc.scalar.activation(wg_hi[:, k], wg[:, k], ACT.Copy).then_inc(wg_hi_ok, 1)
            high_ww(1)
            for j in range(GROUP):
                high_a(j, j, 0)
                if j == 0:
                    act.wait_ge(ld_x[1], 16)
                nc.scalar.activation(x_hi[:, 1, j], x[:, 1, j], ACT.Copy).then_inc(x1_hi, 1)
                if j == 1:
                    act.wait_ge(ld_wc, 16)
                    for e in range(KE):
                        nc.scalar.activation(wc_hi[:, e], wc[:, e], ACT.Copy, scale=0.5).then_inc(wc_hi_ok, 1)
            for g in range(2, G):
                act.wait_ge(ld_x[g], 16)
                nc.scalar.activation(x_hi[:, g], x[:, g], ACT.Copy).then_inc(xs_hi, 1)
            act.wait_ge(bias_halved, 2)
            with act.Fori(1, G) as g:
                read_q(g)
                for j in range(GROUP):
                    b = GROUP * g + j
                    if 0 < j < GROUP - 1:
                        exponentials(b, j)
                        tanh(g - 1, j)
                    else:
                        tanh(g - 1, j)
                        exponentials(b, j)
                    if j < GROUP - 1:
                        high_a(b, j, g % 2)
                        square(g - 1, j)
                        weight(g - 1, j)
                    else:
                        nc.scalar.preload_act_table_set("natural_log_exp_and_others")
                        square(g - 1, j)
                        weight(g - 1, j)
                        root(g)
                        high_a(b, j, g % 2)
            for c in range(KD - 1):
                tanh(G - 1, c)
                square(G - 1, c)
                weight(G - 1, c)
            tanh(G - 1, KD - 1)
            nc.scalar.preload_act_table_set("natural_log_exp_and_others")
            for h, rows in enumerate(HALVES):
                square(G - 1, KD - 1, h, rows)
            for h, rows in enumerate(HALVES):
                weight(G - 1, KD - 1, h, rows)
            for h, rows in enumerate(HALVES):
                root(G + h, [p_logit[0], p_scores][h], rows)

        @block.vector
        def _(dve):
            def low(out, whole, high, ready, done):
                if ready is not None:
                    dve.wait_ge(*ready)
                nc.vector.tensor_tensor(out, whole, f32(high), ALU.subtract).then_inc(done, 1)

            def neg_row_max(b, j, scores=p_scores):
                dve.wait_ge(scores_made, b + 1)
                nc.vector.tensor_reduce(neg_max[0:N, j:j + 1], scores[0:N, 0:M], AX.X, ALU.max,
                                        negate=True).then_inc(max_made, 1)

            def normalise(b, j):
                dve.wait_ge(exp_made, b + 1)
                nc.vector.reciprocal(row_inv[0:N, j:j + 1], row_sum[0:N, j:j + 1]).then_inc(inv_made, 1)
                dve.wait_ge(inv_made, b + 1)
                nc.vector.tensor_scalar(probs[0:N, j], probs[0:N, j], row_inv[0:N, j:j + 1], None,
                                        ALU.mult).then_inc(probs_ready, 1)

            def read_probsT(b, j, bank=p_probsT):
                dve.wait_ge(probsT_made, b + 1)
                full = (MT - 1) * N
                nc.vector.tensor_copy(probsT[:, j % 2, 0:full], bank[:, 0:full])
                nc.vector.tensor_copy(probsT[0:MROWS[-1], j % 2, full:], bank[0:MROWS[-1], full:MT * N])\
                    .then_inc(probsT_ready, 1)

            def low_a(b, j, par):
                dve.wait_ge(aT_hi_ready, b + 1)
                low(aT_lo[:, par, :, j * N:(j + 1) * N], p_aT[:, 0:KE * N].rearrange("p (e n) -> p e n", e=KE),
                    aT_hi[:, par, :, j * N:(j + 1) * N], None, aT_lo_ready)

            def gate_context(g, c, h=0, rows=ALL):
                if not h:
                    dve.wait_ge(tanh_made, KD * g + c + 1)
                dve.wait_ge(ctx_made, KD * g + c + h + 1)
                nc.vector.scalar_tensor_tensor(out=gated[:, c % 2, rows], in0=gated[:, c % 2, rows], scalar=1.0,
                                               in1=p_ctx[(c + h) % 2][:, rows], op0=ALU.add, op1=ALU.mult)\
                    .then_inc(gated_made, 1)
                dve.wait_ge(gated_made, KD * g + c + h + 1)
                nc.vector.tensor_tensor(x[:, g, c, rows], x[:, g, c, rows], gated[:, c % 2, rows], ALU.add)\
                    .then_inc(fused_made, 1)

            def output(g, c, rows=ALL):
                nc.vector.tensor_tensor(x[:, g, c, rows], x[:, g, c, rows], rstd[:, rows], ALU.mult).then_inc(out_made, 1)

            for k in range(KD):
                low(wq_lo[:, k], wq[:, k], wq_hi[:, k], (wq_hi_ok, k + 1), wq_lo_ok)
                low(x_lo[:, 0, k], x[:, 0, k], x_hi[:, 0, k], (x0_hi, k + 1), x0_lo)

            def low_ww(e):
                low(ww_lo[:, e], p_ww[e][:, 0:D], ww_hi[:, e], (ww_hi_ok, e + 1), ww_lo_ok)

            low_ww(0)
            neg_row_max(0, 0, p_scores_first[0])
            for j in range(GROUP):
                if j < GROUP - 1:
                    neg_row_max(j + 1, j + 1, p_scores_first[j + 1])
                normalise(j, j)
            for k in range(KD):
                low(wg_lo[:, k], wg[:, k], wg_hi[:, k], (wg_hi_ok, k + 1), wg_lo_ok)
            for j in range(GROUP + 1):
                if j < GROUP:
                    read_probsT(j, j, p_probsT_first[j])
                if j:
                    low_a(j - 1, j - 1, 0)
                else:
                    low_ww(1)
            for e in range(KE):
                dve.wait_ge(wc_hi_ok, e + 1)
                nc.vector.scalar_tensor_tensor(out=wc_lo[:, e], in0=wc[:, e], scalar=0.5, in1=f32(wc_hi[:, e]),
                                               op0=ALU.mult, op1=ALU.subtract).then_inc(wc_lo_ok, 1)
            dve.wait_ge(ld_bw, 16)
            nc.vector.tensor_scalar(half_b[:, :], bw[:, 0:KD], 0.5, None, ALU.mult).then_inc(bias_halved, 1)
            nc.vector.memset(eps[:, :], EPS).then_inc(bias_halved, 1)
            with dve.Fori(1, G) as g:
                for j in range(GROUP):
                    b = GROUP * g + j
                    if j < GROUP - 1:
                        neg_row_max(b, j)
                        normalise(b, j)
                        gate_context(g - 1, j)
                    else:
                        gate_context(g - 1, j)
                        neg_row_max(b, j)
                        normalise(b, j)
                    read_probsT(b, j)
                    low_a(b, j, g % 2)
                dve.wait_ge(weighted, KD * g)
                dve.wait_ge(rstd_made, g)
                for c in range(DVE_OUT):
                    output(g - 1, c)
            for c in range(KD - 1):
                gate_context(G - 1, c)
            for h, rows in enumerate(HALVES):
                gate_context(G - 1, KD - 1, h, rows)
            for h, rows in enumerate(HALVES):
                dve.wait_ge(sq_added, (KD - 2) * G)
                dve.wait_ge(sq_made, KD * G + h)
                nc.vector.tensor_tensor(sq_sum[:, rows], sq_sum[:, rows], squares[:, (KD - 1) % 2, rows], ALU.add)\
                    .then_inc(sq_sum_made, 1)
            dve.wait_ge(weighted, KD * G + 1)
            for h, rows in enumerate(HALVES):
                dve.wait_ge(rstd_made, G + h)
                for c in range(DVE_OUT):
                    output(G - 1, c, rows)

        @block.gpsimd
        def _(pool):
            nc.gpsimd.memset(mean_of[:, :], 1.0 / D).then_inc(consts, 1)
            nc.gpsimd.memset(ident[:, :], 0.0).then_inc(zeroed, 1)
            pool.wait_ge(zeroed, 1)
            nc.gpsimd.affine_select(out=ident[:, :], in_=ident[:, :], compare_op=ALU.not_equal, fill=1.0, base=0,
                                    pattern=[[-1, N]], channel_multiplier=1).then_inc(consts, 1)
            for k in range(KD):
                pool.wait_ge(x1_hi, k + 1)
                nc.gpsimd.tensor_tensor(x_lo[:, 1, k], x[:, 1, k], f32(x_hi[:, 1, k]), ALU.subtract)\
                    .then_inc(xs_lo if k == KD - 1 else x1_lo, 1)
            for g in range(2, G):
                pool.wait_ge(xs_hi, g - 1)
                nc.gpsimd.tensor_tensor(x_lo[:, g], x[:, g], f32(x_hi[:, g]), ALU.subtract).then_inc(xs_lo, 1)

            def add_squares(g, c):
                pool.wait_ge(sq_made, KD * g + c + 1)
                if c == 1:
                    nc.gpsimd.tensor_tensor(sq_sum[:, :], squares[:, 0], squares[:, 1], ALU.add).then_inc(sq_added, 1)
                else:
                    pool.wait_ge(sq_added, (KD - 2) * g + c - 1)
                    nc.gpsimd.tensor_tensor(sq_sum[:, :], sq_sum[:, :], squares[:, c % 2], ALU.add)\
                        .then_inc(sq_added if c < KD - 1 else sq_sum_made, 1)

            with pool.Fori(0, G - 1) as g:
                for c in range(1, KD):
                    add_squares(g, c)
                pool.wait_ge(weighted, KD * g + KD)
                pool.wait_ge(rstd_made, g + 1)
                for c in range(DVE_OUT, KD):
                    nc.gpsimd.tensor_tensor(x[:, g, c], x[:, g, c], rstd[:, :], ALU.mult).then_inc(pool_out_made, 1)
            for c in range(1, KD - 1):
                add_squares(G - 1, c)
            pool.wait_ge(weighted, KD * G + 1)
            for h, rows in enumerate(HALVES):
                pool.wait_ge(rstd_made, G + h)
                for c in range(DVE_OUT, KD):
                    nc.gpsimd.tensor_tensor(x[:, G - 1, c, rows], x[:, G - 1, c, rows], rstd[:, rows], ALU.mult)\
                        .then_inc(pool_out_made, 1)


_INS = ["x", "ctx_1024", "L0_xattn_W_mem", "L0_xattn_W_gate", "L0_xattn_b_gate", "L0_xattn_norm_w"]


def kernel(**inputs):
    import numpy as np
    import concourse.bacc as bacc
    from concourse.bass_utils import run_bass_kernel_spmd as run

    x, mem, w_mem, w_gate, b_gate, norm_w = (np.asarray(inputs[n]) for n in _INS)

    def lay(a):
        return np.ascontiguousarray(a)

    padded = np.zeros((B, MT * P, E), mem.dtype)
    padded[:, :M] = mem
    arrays = {
        "xT": lay(x.reshape(G, NG, KD, P).transpose(0, 3, 2, 1)),
        "memT": lay(mem.reshape(B, M, KE, P).transpose(0, 3, 2, 1)).reshape(B, P, KE * M),
        "memN": lay(padded.reshape(B, MT, P, E).transpose(0, 2, 1, 3)).reshape(B, P, MT * E),
        "w_mem": lay(w_mem.reshape(KD, P, E).transpose(1, 0, 2)),
        "w_memT": lay(w_mem.reshape(D, KE, P).transpose(2, 1, 0)),
        "w_gateT": lay(w_gate.reshape(D, 2 * KD, P).transpose(2, 1, 0)),
        "vecs": lay(np.concatenate([b_gate.reshape(KD, P), norm_w.reshape(KD, P)]).transpose()),
    }
    nc = bacc.Bacc("TRN2", target_bir_lowering=False, num_devices=1)
    args = [nc.dram_tensor(n, a.shape, mybir.dt.from_np(a.dtype), kind="ExternalInput").ap() for n, a in arrays.items()]
    out = nc.dram_tensor("outT", (G, P, KD, NG), F32, kind="ExternalOutput").ap()
    build(nc, *args, out)
    r = run(nc, [arrays], core_ids=[0])
    return r.results[0]["outT"].transpose(0, 3, 2, 1).reshape(B, N, D)
```

```python
from contextlib import ExitStack

import concourse.bass as bass
from concourse import mybir

ALU = mybir.AluOpType
ACT = mybir.ActivationFunctionType
AX = mybir.AxisListType
F32 = mybir.dt.float32
F32R = mybir.dt.float32r

P = 128
B, N, M, D, E = 16, 112, 375, 512, 256
GROUP = 4
G = B // GROUP
NG = GROUP * N
KD, KE = D // P, E // P
M2 = M + M % 2
MT = -(-M // P)
MROWS = [min(P, M - P * t) for t in range(MT)]
SCORE_SCALE = float(D) ** -0.5
EPS = 1e-6
WARM_UP = 8
DVE_OUT = KD - 1
HALVES = [slice(0, NG // 2), slice(NG // 2, NG)]
ALL = slice(0, NG)


def build(nc: bass.Bass, xT, memT, memN, w_mem, w_memT, w_gateT, vecs, outT):
    with ExitStack() as ctx:
        def sb(name, shape, dt=F32):
            return ctx.enter_context(nc.sbuf_tensor(name, shape, dt))

        def bank(name):
            return ctx.enter_context(nc.psum_tensor(name, [P, 512], F32))

        def sem(name):
            return ctx.enter_context(nc.semaphore(name))

        x = sb("x", [P, G, KD, NG])
        x_hi = sb("x_hi", [P, G, KD, NG], F32R)
        x_lo = sb("x_lo", [P, G, KD, NG], F32R)
        wq = sb("wq", [P, KD, E])
        wq_hi = sb("wq_hi", [P, KD, E], F32R)
        wq_lo = sb("wq_lo", [P, KD, E], F32R)
        wc = sb("wc", [P, KE, D])
        wc_hi = sb("wc_hi", [P, KE, D], F32R)
        wc_lo = sb("wc_lo", [P, KE, D], F32R)
        wg = sb("wg", [P, 2 * KD, D])
        wg_hi = sb("wg_hi", [P, KD, D], F32R)
        wg_lo = sb("wg_lo", [P, KD, D], F32R)
        ww_hi = sb("ww_hi", [P, KE, D], F32R)
        ww_lo = sb("ww_lo", [P, KE, D], F32R)
        bw = sb("bw", [P, 2 * KD])
        half_b = sb("half_b", [P, KD])
        ident = sb("ident", [N, N])
        mean_of = sb("mean_of", [P, P])
        mem_t = sb("mem_t", [P, 2, KE * M2])
        mem_t_hi = sb("mem_t_hi", [P, 2, KE * M2], F32R)
        mem_t_lo = sb("mem_t_lo", [P, 2, KE * M2], F32R)
        mem_n = sb("mem_n", [P, GROUP, MT * E])
        q_hi = sb("q_hi", [P, KE, NG], F32R)
        q_lo = sb("q_lo", [P, KE, NG], F32R)
        neg_max = sb("neg_max", [P, GROUP])
        row_sum = sb("row_sum", [P, GROUP])
        row_inv = sb("row_inv", [P, GROUP])
        probs = sb("probs", [P, GROUP, M])
        aT_hi = sb("aT_hi", [P, 2, KE, NG], F32R)
        aT_lo = sb("aT_lo", [P, 2, KE, NG], F32R)
        spent = wg[:, KD:].rearrange("p k d -> p (k d)")
        gated = spent[:, 0:2 * NG].rearrange("p (s n) -> p s n", s=2)
        squares = spent[:, 2 * NG:4 * NG].rearrange("p (s n) -> p s n", s=2)
        split = wg[:, 0:KD].rearrange("p k d -> p (k d)")
        sq_sum, rstd = split[:, 0:NG], split[:, NG:2 * NG]
        probsT = wq[:, :, :].rearrange("p k e -> p (k e)")[:, 0:2 * MT * N].rearrange("p (s n) -> p s n", s=2)
        eps = sb("eps", [P, 1])

        p_scores = bank("p_scores")
        p_probsT = bank("p_probsT")
        p_aT = bank("p_aT")
        p_q0 = bank("p_q0")
        p_logit = [bank("p_logit0"), bank("p_logit1")]
        p_ctx = [bank("p_ctx0"), bank("p_ctx1")]
        p_q = [p_q0, p_aT]
        p_scores_first = [p_scores, p_ctx[0], p_ctx[1], p_logit[1]]
        p_ww = [p_logit[0], p_q0]
        p_probsT_first = [p_probsT, p_scores, p_ctx[0], p_ctx[1]]
        p_aT_first = [p_aT, p_logit[1]] * (GROUP // 2)

        ld_x = [sem(f"ld_x_{g}") for g in range(G)]
        ld_x0 = [sem(f"ld_x0_{k}") for k in range(KD)]
        ld_wq = [sem(f"ld_wq_{k}") for k in range(KD)]
        ld_wc, ld_wg1, ld_wg2, ld_bw = (sem(n) for n in ("ld_wc", "ld_wg1", "ld_wg2", "ld_bw"))
        ld_memT = [sem(f"ld_memT{j}") for j in range(GROUP)]
        ld_memN = [sem(f"ld_memN{j}") for j in range(GROUP)]
        stored = sem("stored")
        zeroed, consts, bias_halved = sem("zeroed"), sem("consts"), sem("bias_halved")
        x0_hi, x0_lo, x1_hi, xs_hi, x1_lo, xs_lo = (sem(n) for n in ("x0_hi", "x0_lo", "x1_hi", "xs_hi", "x1_lo", "xs_lo"))
        wq_hi_ok, wq_lo_ok = sem("wq_hi_ok"), sem("wq_lo_ok")
        wc_hi_ok, wc_lo_ok = sem("wc_hi_ok"), sem("wc_lo_ok")
        wg_hi_ok, wg_lo_ok = sem("wg_hi_ok"), sem("wg_lo_ok")
        ww_made, ww_hi_ok, ww_lo_ok = sem("ww_made"), sem("ww_hi_ok"), sem("ww_lo_ok")
        q_made, q_hi_ready, q_ready = sem("q_made"), sem("q_hi_ready"), sem("q_ready")
        memT_hi_ready, memT_ready = sem("memT_hi_ready"), sem("memT_ready")
        scores_made, max_made, exp_made, inv_made, probs_ready = (
            sem(n) for n in ("scores_made", "max_made", "exp_made", "inv_made", "probs_ready"))
        probsT_made, probsT_ready = sem("probsT_made"), sem("probsT_ready")
        aT_made, aT_hi_ready, aT_lo_ready = sem("aT_made"), sem("aT_hi_ready"), sem("aT_lo_ready")
        logit_made, ctx_made, tanh_made, gated_made, fused_made, sq_made = (
            sem(n) for n in ("logit_made", "ctx_made", "tanh_made", "gated_made", "fused_made", "sq_made"))
        sq_added, weighted = sem("sq_added"), sem("weighted")
        sq_sum_made, mean_made, log_made, rstd_made, out_made, pool_out_made = (
            sem(n) for n in ("sq_sum_made", "mean_made", "log_made", "rstd_made", "out_made", "pool_out_made"))

        def f32(ap):
            return ap.bitcast(F32)

        block = ctx.enter_context(nc.Block())

        @block.sync
        def _(sp):
            def load_memT(b, j):
                if not (isinstance(b, int) and b < 2):
                    sp.wait_ge(memT_ready, b - 1)
                sp.dma_start(mem_t[:, j % 2, :], memT[b]).then_inc(ld_memT[j], 16)

            def load_memN(b, j):
                sp.dma_start(mem_n[:, j, :], memN[b]).then_inc(ld_memN[j], 16)

            for k in range(KD):
                sp.dma_start(wq[:, k], w_mem[:, k]).then_inc(ld_wq[k], 16)
                sp.dma_start(x[:, 0, k], xT[0, :, k]).then_inc(ld_x0[k], 16)
            sp.dma_start(wg[:, KD:], w_gateT[:, KD:]).then_inc(ld_wg2, 16)
            for j in range(2):
                load_memT(j, j)
            for j in range(2, GROUP):
                load_memT(j, j)
            sp.dma_start(wg[:, 0:KD], w_gateT[:, 0:KD]).then_inc(ld_wg1, 16)
            for j in range(GROUP):
                load_memN(j, j)
            sp.dma_start(wc[:, :, :], w_memT).then_inc(ld_wc, 16)
            sp.dma_start(bw[:, :], vecs).then_inc(ld_bw, 16)
            for g in range(1, G):
                sp.dma_start(x[:, g], xT[g]).then_inc(ld_x[g], 16)
            with sp.Fori(1, G) as g:
                for j in range(GROUP):
                    sp.wait_ge(aT_made, GROUP * g + (j - GROUP + 1))
                    load_memN(GROUP * g + j, j)
                    load_memT(GROUP * g + j, j)
            with sp.Fori(0, G - 1) as g:
                for c in range(KD):
                    if c < DVE_OUT:
                        sp.wait_ge(out_made, DVE_OUT * g + c + 1)
                    else:
                        sp.wait_ge(pool_out_made, (KD - DVE_OUT) * g + c - DVE_OUT + 1)
                    sp.dma_start(outT[g, :, c], x[:, g, c]).then_inc(stored, 16)
            for h, rows in enumerate(HALVES):
                sp.wait_ge(out_made, DVE_OUT * (G + h))
                sp.dma_start(outT[G - 1, :, 0:DVE_OUT, rows], x[:, G - 1, 0:DVE_OUT, rows]).then_inc(stored, 16)
                sp.wait_ge(pool_out_made, (KD - DVE_OUT) * (G + h))
                sp.dma_start(outT[G - 1, :, DVE_OUT:, rows], x[:, G - 1, DVE_OUT:, rows]).then_inc(stored, 16)
            sp.wait_ge(stored, 16 * (KD * (G - 1) + 2 * len(HALVES)))

        @block.tensor
        def _(pe):
            def three(out, w_hi, w_lo, m_hi, m_lo, first, last):
                pe.matmul(out, w_hi, m_hi, start=first, stop=False)
                pe.matmul(out, w_lo, m_hi, start=False, stop=False)
                return pe.matmul(out, w_hi, m_lo, start=False, stop=last)

            def q_part(g, e, k):
                return three(p_q[e][:, 0:NG], wq_hi[:, k, e * P:(e + 1) * P], wq_lo[:, k, e * P:(e + 1) * P],
                             x_hi[:, g, k], x_lo[:, g, k], k == 0, k == KD - 1)

            def product_of_weights(e):
                for k in range(KD):
                    mm = pe.matmul(p_ww[e][:, 0:D], wq[:, k, e * P:(e + 1) * P], wg[:, KD + k],
                                   start=(k == 0), stop=(k == KD - 1))
                mm.then_inc(ww_made, 1)

            def score(b, j, into=p_scores):
                pe.wait_ge(memT_ready, b + 1)
                for e in range(KE):
                    cols = slice(e * M2, (e + 1) * M2)
                    mm = three(into[0:N, 0:M2], q_hi[:, e, j * N:(j + 1) * N], q_lo[:, e, j * N:(j + 1) * N],
                               mem_t_hi[:, j % 2, cols], mem_t_lo[:, j % 2, cols], e == 0, e == KE - 1)
                mm.then_inc(scores_made, 1)

            def transpose_probs(b, j, into=p_probsT):
                pe.wait_ge(probs_ready, b + 1)
                for t in range(MT):
                    mm = pe.transpose(into[0:MROWS[t], t * N:(t + 1) * N],
                                      probs[0:N, j, t * P:t * P + MROWS[t]], ident[:, :])
                mm.then_inc(probsT_made, 1)

            def attend(b, j, into=p_aT):
                pe.wait_ge(probsT_ready, b + 1)
                pe.wait_ge(ld_memN[j], 16 * (b // GROUP + 1) if isinstance(b, int) else b * 4 + (16 - 4 * j))
                for e in range(KE):
                    for t in range(MT):
                        mm = pe.matmul(into[:, e * N:(e + 1) * N],
                                       mem_n[0:MROWS[t], j, t * E + e * P:t * E + (e + 1) * P],
                                       probsT[0:MROWS[t], j % 2, t * N:(t + 1) * N],
                                       start=(t == 0), stop=(t == MT - 1))
                mm.then_inc(aT_made, 1)

            def logits_from_x(g, c, ks=range(KD)):
                for k in ks:
                    mm = three(p_logit[c % 2][:, 0:NG], wg_hi[:, k, c * P:(c + 1) * P],
                               wg_lo[:, k, c * P:(c + 1) * P], x_hi[:, g, k], x_lo[:, g, k], k == 0, False)
                return mm

            def logits_from_a(g, c, par):
                for e in range(KE):
                    mm = three(p_logit[c % 2][:, 0:NG], ww_hi[:, e, c * P:(c + 1) * P],
                               ww_lo[:, e, c * P:(c + 1) * P], aT_hi[:, par, e], aT_lo[:, par, e],
                               False, e == KE - 1)
                mm.then_inc(logit_made, 1)

            def context(g, c, par, into=None, rows=ALL):
                into = into or p_ctx[c % 2]
                for e in range(KE):
                    mm = three(into[:, rows], wc_hi[:, e, c * P:(c + 1) * P], wc_lo[:, e, c * P:(c + 1) * P],
                               aT_hi[:, par, e, rows], aT_lo[:, par, e, rows], e == 0, e == KE - 1)
                mm.then_inc(ctx_made, 1)

            def mean_square(count, into=p_logit[1], rows=ALL):
                pe.wait_ge(sq_sum_made, count)
                pe.matmul(into[:, rows], mean_of[:, :], sq_sum[:, rows], start=True, stop=True).then_inc(mean_made, 1)

            pe.wait_ge(consts, 1)
            for _ in range(WARM_UP):
                pe.matmul(p_scores[:, 0:P], mean_of[:, :], mean_of[:, :], start=True, stop=True)

            for k in range(KD):
                pe.wait_ge(wq_lo_ok, k + 1)
                pe.wait_ge(x0_lo, k + 1)
                for e in range(KE):
                    mm = q_part(0, e, k)
                    if k == KD - 1:
                        mm.then_inc(q_made, 1)
            pe.wait_ge(ld_wg2, 16)
            product_of_weights(0)
            pe.wait_ge(q_ready, KE)
            for j in range(GROUP):
                score(j, j, p_scores_first[j])
                if j == 1:
                    product_of_weights(1)
            pe.wait_ge(consts, 2)
            pe.wait_ge(ww_lo_ok, 1)
            for j in range(GROUP + 1):
                if j < GROUP:
                    transpose_probs(j, j, p_probsT_first[j])
                    pe.wait_ge(wg_lo_ok, j + 1)
                    logits_from_x(0, 0, [j])
                if j:
                    if j == 2:
                        pe.wait_ge(exp_made, GROUP)
                    if j > 2:
                        pe.wait_ge(aT_lo_ready, j - 2)
                    attend(j - 1, j - 1, p_aT_first[j - 1])
            pe.wait_ge(ww_lo_ok, KE)

            with pe.Fori(1, G) as g:
                par = (g + 1) % 2
                b = GROUP * g
                pe.wait_ge(xs_lo, g)
                for e in range(KE):
                    if e:
                        pe.wait_ge(aT_lo_ready, b)
                    for k in range(KD):
                        mm = q_part(g, e, k)
                    mm.then_inc(q_made, 1)
                pe.wait_ge(wc_lo_ok, KE)
                logits_from_a(g - 1, 0, par)
                context(g - 1, 0, par)
                pe.wait_ge(q_ready, KE * g + KE)
                score(b, 0)
                logits_from_x(g - 1, 1)
                for j in range(GROUP):
                    if j == GROUP - 1:
                        logits_from_x(g, 0, range(KD // 2))
                    transpose_probs(b + j, j)
                    if j < GROUP - 2:
                        score(b + j + 1, j + 1)
                        attend(b + j, j)
                    if j < GROUP - 1:
                        logits_from_a(g - 1, j + 1, par)
                        if j == GROUP - 2:
                            score(b + j + 1, j + 1)
                        if j:
                            pe.wait_ge(gated_made, KD * g + (j - KD))
                        context(g - 1, j + 1, par)
                    if j < GROUP - 2:
                        pe.wait_ge(tanh_made, KD * g + (j + 1 - KD))
                        logits_from_x(g - 1, j + 2)
                    if j == GROUP - 2:
                        attend(b + j, j)
                        pe.wait_ge(tanh_made, KD * g + (j + 1 - KD))
                    if j == GROUP - 1:
                        logits_from_x(g, 0, range(KD // 2, KD))
                        pe.wait_ge(aT_lo_ready, b + j)
                        attend(b + j, j)
                        mean_square(g)

            par = (G - 1) % 2
            first = KD * (G - 1)
            pe.wait_ge(log_made, G - 1)
            logits_from_x(G - 1, 1)
            pe.wait_ge(aT_lo_ready, B)
            for c in range(KD):
                logits_from_a(G - 1, c, par)
                if c >= 2:
                    pe.wait_ge(gated_made, first + c - 1)
                if c < KD - 1:
                    context(G - 1, c, par)
                if 1 <= c < KD - 1:
                    pe.wait_ge(tanh_made, first + c)
                    logits_from_x(G - 1, c + 1)
            for h, rows in enumerate(HALVES):
                if h == 1:
                    pe.wait_ge(gated_made, first + KD - 1)
                context(G - 1, KD - 1, par, p_ctx[(KD - 1 + h) % 2], rows)
            for h, rows in enumerate(HALVES):
                mean_square(G + h, [p_logit[0], p_scores][h], rows)

        @block.scalar
        def _(act):
            def exponentials(b, j, scores=p_scores):
                act.wait_ge(max_made, b + 1)
                nc.scalar.activation(probs[0:N, j], scores[0:N, 0:M], ACT.Exp, bias=neg_max[0:N, j:j + 1],
                                     accum_out=row_sum[0:N, j:j + 1]).then_inc(exp_made, 1)

            def read_q(g):
                for e in range(KE):
                    act.wait_ge(q_made, KE * g + e + 1)
                    nc.scalar.activation(q_hi[:, e], p_q[e][:, 0:NG], ACT.Copy, scale=SCORE_SCALE).then_inc(q_hi_ready, 1)

            def high_memory(b, j):
                if isinstance(b, int):
                    if b >= 2:
                        act.wait_ge(scores_made, b - 1)
                    act.wait_ge(ld_memT[j], 16)
                else:
                    act.wait_ge(ld_memT[j], GROUP * b + (16 - GROUP * j))
                nc.scalar.activation(mem_t_hi[:, j % 2], mem_t[:, j % 2], ACT.Copy).then_inc(memT_hi_ready, 1)

            def high_a(b, j, par, bank=p_aT):
                act.wait_ge(aT_made, b + 1)
                nc.scalar.activation(aT_hi[:, par, :, j * N:(j + 1) * N],
                                     bank[:, 0:KE * N].rearrange("p (e n) -> p e n", e=KE),
                                     ACT.Copy).then_inc(aT_hi_ready, 1)

            def tanh(g, c):
                act.wait_ge(logit_made, KD * g + c + 1)
                nc.scalar.activation(gated[:, c % 2], p_logit[c % 2][:, 0:NG], ACT.Tanh, bias=half_b[:, c:c + 1],
                                     scale=0.5).then_inc(tanh_made, 1)

            def square(g, c, h=0, rows=ALL):
                act.wait_ge(fused_made, KD * g + c + h + 1)
                if c >= 2:
                    act.wait_ge(sq_added, (KD - 2) * g + 1)
                nc.scalar.activation(squares[:, c % 2, rows], x[:, g, c, rows], ACT.Square).then_inc(sq_made, 1)

            def weight(g, c, h=0, rows=ALL):
                nc.scalar.activation(x[:, g, c, rows], x[:, g, c, rows], ACT.Copy,
                                     scale=bw[:, KD + c:KD + c + 1]).then_inc(weighted, 1)

            def root(count, mean=p_logit[1], rows=ALL):
                act.wait_ge(mean_made, count)
                nc.scalar.activation(rstd[:, rows], mean[:, rows], ACT.Ln, bias=eps[:, 0:1]).then_inc(log_made, 1)
                act.wait_ge(log_made, count)
                nc.scalar.activation(rstd[:, rows], rstd[:, rows], ACT.Exp, scale=-0.5).then_inc(rstd_made, 1)

            for k in range(KD):
                act.wait_ge(ld_wq[k], 16)
                nc.scalar.activation(wq_hi[:, k], wq[:, k], ACT.Copy).then_inc(wq_hi_ok, 1)
                act.wait_ge(ld_x0[k], 16)
                nc.scalar.activation(x_hi[:, 0, k], x[:, 0, k], ACT.Copy).then_inc(x0_hi, 1)
            high_memory(0, 0)
            high_memory(1, 1)
            read_q(0)

            def high_ww(e):
                act.wait_ge(ww_made, e + 1)
                nc.scalar.activation(ww_hi[:, e], p_ww[e][:, 0:D], ACT.Copy).then_inc(ww_hi_ok, 1)

            high_ww(0)
            for j in range(GROUP):
                if j == 1:
                    high_memory(2, 2)
                    high_memory(3, 3)
                exponentials(j, j, p_scores_first[j])
                if j == 1:
                    act.wait_ge(ld_wg1, 16)
                    for k in range(KD):
                        nc.scalar.activation(wg_hi[:, k], wg[:, k], ACT.Copy).then_inc(wg_hi_ok, 1)
                    high_ww(1)
            for j in range(GROUP):
                high_a(j, j, 0, p_aT_first[j])
                if j == 0:
                    act.wait_ge(ld_x[1], 16)
                for k in range(2 * j, min(2 * j + 2, KD)):
                    nc.scalar.activation(x_hi[:, 1, k], x[:, 1, k], ACT.Copy).then_inc(x1_hi, 1)
                if j == 2:
                    act.wait_ge(ld_wc, 16)
                    for e in range(KE):
                        nc.scalar.activation(wc_hi[:, e], wc[:, e], ACT.Copy, scale=0.5).then_inc(wc_hi_ok, 1)
            act.wait_ge(bias_halved, 2)
            with act.Fori(1, G) as g:
                b = GROUP * g
                high_memory(b, 0)
                read_q(g)
                tanh(g - 1, 0)
                high_memory(b + 1, 1)
                for j in range(GROUP):
                    exponentials(b + j, j)
                    if j == GROUP - 1:
                        tanh(g - 1, j)
                        high_a(b + j - 1, j - 1, g % 2)
                        square(g - 1, j)
                    if 0 < j < GROUP - 1:
                        high_a(b + j - 1, j - 1, g % 2)
                        tanh(g - 1, j)
                    if j < GROUP - 1:
                        square(g - 1, j)
                    weight(g - 1, j)
                    if j < GROUP - 2:
                        high_memory(b + j + 2, j + 2)
                nc.scalar.preload_act_table_set("natural_log_exp_and_others")
                high_a(b + GROUP - 1, GROUP - 1, g % 2)
                root(g)
            for c in range(KD - 1):
                tanh(G - 1, c)
                square(G - 1, c)
                weight(G - 1, c)
            tanh(G - 1, KD - 1)
            nc.scalar.preload_act_table_set("natural_log_exp_and_others")
            for h, rows in enumerate(HALVES):
                square(G - 1, KD - 1, h, rows)
            for h, rows in enumerate(HALVES):
                weight(G - 1, KD - 1, h, rows)
            for h, rows in enumerate(HALVES):
                root(G + h, [p_logit[0], p_scores][h], rows)

        @block.vector
        def _(dve):
            def low(out, whole, high, ready, done):
                if ready is not None:
                    dve.wait_ge(*ready)
                nc.vector.tensor_tensor(out, whole, f32(high), ALU.subtract).then_inc(done, 1)

            def neg_row_max(b, j, scores=p_scores):
                dve.wait_ge(scores_made, b + 1)
                nc.vector.tensor_reduce(neg_max[0:N, j:j + 1], scores[0:N, 0:M], AX.X, ALU.max,
                                        negate=True).then_inc(max_made, 1)

            def normalise(b, j):
                dve.wait_ge(exp_made, b + 1)
                nc.vector.reciprocal(row_inv[0:N, j:j + 1], row_sum[0:N, j:j + 1]).then_inc(inv_made, 1)
                dve.wait_ge(inv_made, b + 1)
                nc.vector.tensor_scalar(probs[0:N, j], probs[0:N, j], row_inv[0:N, j:j + 1], None,
                                        ALU.mult).then_inc(probs_ready, 1)

            def read_probsT(b, j, bank=p_probsT):
                dve.wait_ge(probsT_made, b + 1)
                full = (MT - 1) * N
                nc.vector.tensor_copy(probsT[:, j % 2, 0:full], bank[:, 0:full])
                nc.vector.tensor_copy(probsT[0:MROWS[-1], j % 2, full:], bank[0:MROWS[-1], full:MT * N])\
                    .then_inc(probsT_ready, 1)

            def low_q(g):
                for e in range(KE):
                    dve.wait_ge(q_hi_ready, KE * g + e + 1)
                    nc.vector.scalar_tensor_tensor(out=q_lo[:, e], in0=p_q[e][:, 0:NG], scalar=SCORE_SCALE,
                                                   in1=f32(q_hi[:, e]), op0=ALU.mult, op1=ALU.subtract)\
                        .then_inc(q_ready, 1)

            def low_memory(b, j):
                low(mem_t_lo[:, j % 2], mem_t[:, j % 2], mem_t_hi[:, j % 2], (memT_hi_ready, b + 1), memT_ready)

            def low_a(b, j, par, bank=p_aT):
                dve.wait_ge(aT_hi_ready, b + 1)
                low(aT_lo[:, par, :, j * N:(j + 1) * N], bank[:, 0:KE * N].rearrange("p (e n) -> p e n", e=KE),
                    aT_hi[:, par, :, j * N:(j + 1) * N], None, aT_lo_ready)

            def gate_context(g, c, h=0, rows=ALL):
                if not h:
                    dve.wait_ge(tanh_made, KD * g + c + 1)
                dve.wait_ge(ctx_made, KD * g + c + h + 1)
                nc.vector.scalar_tensor_tensor(out=gated[:, c % 2, rows], in0=gated[:, c % 2, rows], scalar=1.0,
                                               in1=p_ctx[(c + h) % 2][:, rows], op0=ALU.add, op1=ALU.mult)\
                    .then_inc(gated_made, 1)
                dve.wait_ge(gated_made, KD * g + c + h + 1)
                nc.vector.tensor_tensor(x[:, g, c, rows], x[:, g, c, rows], gated[:, c % 2, rows], ALU.add)\
                    .then_inc(fused_made, 1)

            def output(g, c, rows=ALL):
                nc.vector.tensor_tensor(x[:, g, c, rows], x[:, g, c, rows], rstd[:, rows], ALU.mult).then_inc(out_made, 1)

            for k in range(KD):
                low(wq_lo[:, k], wq[:, k], wq_hi[:, k], (wq_hi_ok, k + 1), wq_lo_ok)
                low(x_lo[:, 0, k], x[:, 0, k], x_hi[:, 0, k], (x0_hi, k + 1), x0_lo)

            low_memory(0, 0)
            low_memory(1, 1)
            low_q(0)

            def low_ww(e):
                low(ww_lo[:, e], p_ww[e][:, 0:D], ww_hi[:, e], (ww_hi_ok, e + 1), ww_lo_ok)

            def low_wg(k):
                low(wg_lo[:, k], wg[:, k], wg_hi[:, k], (wg_hi_ok, k + 1), wg_lo_ok)

            low_ww(0)
            neg_row_max(0, 0, p_scores_first[0])
            neg_row_max(1, 1, p_scores_first[1])
            normalise(0, 0)
            low_memory(2, 2)
            low_memory(3, 3)
            normalise(1, 1)
            low_wg(0)
            low_wg(1)
            neg_row_max(2, 2, p_scores_first[2])
            low_wg(2)
            neg_row_max(3, 3, p_scores_first[3])
            read_probsT(0, 0, p_probsT_first[0])
            normalise(2, 2)
            low_wg(3)
            read_probsT(1, 1, p_probsT_first[1])
            normalise(3, 3)
            low_ww(1)
            for j in range(GROUP):
                low_a(j, j, 0, p_aT_first[j])
                if j < GROUP - 2:
                    read_probsT(j + 2, j + 2, p_probsT_first[j + 2])
            for e in range(KE):
                dve.wait_ge(wc_hi_ok, e + 1)
                nc.vector.scalar_tensor_tensor(out=wc_lo[:, e], in0=wc[:, e], scalar=0.5, in1=f32(wc_hi[:, e]),
                                               op0=ALU.mult, op1=ALU.subtract).then_inc(wc_lo_ok, 1)
            dve.wait_ge(ld_bw, 16)
            nc.vector.tensor_scalar(half_b[:, :], bw[:, 0:KD], 0.5, None, ALU.mult).then_inc(bias_halved, 1)
            nc.vector.memset(eps[:, :], EPS).then_inc(bias_halved, 1)
            with dve.Fori(1, G) as g:
                b = GROUP * g
                low_memory(b, 0)
                low_q(g)
                gate_context(g - 1, 0)
                neg_row_max(b, 0)
                low_memory(b + 1, 1)
                for j in range(GROUP):
                    if j < GROUP - 1:
                        normalise(b + j, j)
                    if 0 < j < GROUP - 1:
                        gate_context(g - 1, j)
                    read_probsT(b + j, j)
                    if j < GROUP - 1:
                        neg_row_max(b + j + 1, j + 1)
                    if j < GROUP - 2:
                        low_memory(b + j + 2, j + 2)
                    if j == GROUP - 2:
                        normalise(b + j + 1, j + 1)
                        gate_context(g - 1, j + 1)
                    low_a(b + j, j, g % 2)
                dve.wait_ge(weighted, KD * g)
                dve.wait_ge(rstd_made, g)
                for c in range(DVE_OUT):
                    output(g - 1, c)
            for c in range(KD - 1):
                gate_context(G - 1, c)
            for h, rows in enumerate(HALVES):
                gate_context(G - 1, KD - 1, h, rows)
            for h, rows in enumerate(HALVES):
                dve.wait_ge(sq_added, (KD - 2) * G)
                dve.wait_ge(sq_made, KD * G + h)
                nc.vector.tensor_tensor(sq_sum[:, rows], sq_sum[:, rows], squares[:, (KD - 1) % 2, rows], ALU.add)\
                    .then_inc(sq_sum_made, 1)
            dve.wait_ge(weighted, KD * G + 1)
            for h, rows in enumerate(HALVES):
                dve.wait_ge(rstd_made, G + h)
                for c in range(DVE_OUT):
                    output(G - 1, c, rows)

        @block.gpsimd
        def _(pool):
            nc.gpsimd.memset(mean_of[:, :], 1.0 / D).then_inc(consts, 1)
            nc.gpsimd.memset(ident[:, :], 0.0).then_inc(zeroed, 1)
            pool.wait_ge(zeroed, 1)
            nc.gpsimd.affine_select(out=ident[:, :], in_=ident[:, :], compare_op=ALU.not_equal, fill=1.0, base=0,
                                    pattern=[[-1, N]], channel_multiplier=1).then_inc(consts, 1)
            for k in range(KD):
                pool.wait_ge(x1_hi, k + 1)
                nc.gpsimd.tensor_tensor(x_lo[:, 1, k], x[:, 1, k], f32(x_hi[:, 1, k]), ALU.subtract)\
                    .then_inc(xs_lo if k == KD - 1 else x1_lo, 1)

            def split_x(g):
                pool.wait_ge(ld_x[g], 16)
                nc.gpsimd.tensor_copy(x_hi[:, g], x[:, g]).then_inc(xs_hi, 1)
                pool.wait_ge(xs_hi, g - 1)
                nc.gpsimd.tensor_tensor(x_lo[:, g], x[:, g], f32(x_hi[:, g]), ALU.subtract).then_inc(xs_lo, 1)

            split_x(2)

            def add_squares(g, c):
                pool.wait_ge(sq_made, KD * g + c + 1)
                if c == 1:
                    nc.gpsimd.tensor_tensor(sq_sum[:, :], squares[:, 0], squares[:, 1], ALU.add).then_inc(sq_added, 1)
                else:
                    pool.wait_ge(sq_added, (KD - 2) * g + c - 1)
                    nc.gpsimd.tensor_tensor(sq_sum[:, :], sq_sum[:, :], squares[:, c % 2], ALU.add)\
                        .then_inc(sq_added if c < KD - 1 else sq_sum_made, 1)

            def finish(g):
                for c in range(1, KD):
                    add_squares(g, c)
                pool.wait_ge(weighted, KD * g + KD)
                pool.wait_ge(rstd_made, g + 1)
                for c in range(DVE_OUT, KD):
                    nc.gpsimd.tensor_tensor(x[:, g, c], x[:, g, c], rstd[:, :], ALU.mult).then_inc(pool_out_made, 1)

            finish(0)
            for g in range(3, G):
                split_x(g)
            with pool.Fori(1, G - 1) as g:
                finish(g)
            for c in range(1, KD - 1):
                add_squares(G - 1, c)
            pool.wait_ge(weighted, KD * G + 1)
            for h, rows in enumerate(HALVES):
                pool.wait_ge(rstd_made, G + h)
                for c in range(DVE_OUT, KD):
                    nc.gpsimd.tensor_tensor(x[:, G - 1, c, rows], x[:, G - 1, c, rows], rstd[:, rows], ALU.mult)\
                        .then_inc(pool_out_made, 1)


_INS = ["x", "ctx_1024", "L0_xattn_W_mem", "L0_xattn_W_gate", "L0_xattn_b_gate", "L0_xattn_norm_w"]


def kernel(**inputs):
    import numpy as np
    import concourse.bacc as bacc
    from concourse.bass_utils import run_bass_kernel_spmd as run

    x, mem, w_mem, w_gate, b_gate, norm_w = (np.asarray(inputs[n]) for n in _INS)

    def lay(a):
        return np.ascontiguousarray(a)

    padded = np.zeros((B, MT * P, E), mem.dtype)
    padded[:, :M] = mem
    arrays = {
        "xT": lay(x.reshape(G, NG, KD, P).transpose(0, 3, 2, 1)),
        "memT": lay(padded[:, :M2].reshape(B, M2, KE, P).transpose(0, 3, 2, 1)).reshape(B, P, KE * M2),
        "memN": lay(padded.reshape(B, MT, P, E).transpose(0, 2, 1, 3)).reshape(B, P, MT * E),
        "w_mem": lay(w_mem.reshape(KD, P, E).transpose(1, 0, 2)),
        "w_memT": lay(w_mem.reshape(D, KE, P).transpose(2, 1, 0)),
        "w_gateT": lay(w_gate.reshape(D, 2 * KD, P).transpose(2, 1, 0)),
        "vecs": lay(np.concatenate([b_gate.reshape(KD, P), norm_w.reshape(KD, P)]).transpose()),
    }
    nc = bacc.Bacc("TRN2", target_bir_lowering=False, num_devices=1)
    args = [nc.dram_tensor(n, a.shape, mybir.dt.from_np(a.dtype), kind="ExternalInput").ap() for n, a in arrays.items()]
    out = nc.dram_tensor("outT", (G, P, KD, NG), F32, kind="ExternalOutput").ap()
    build(nc, *args, out)
    r = run(nc, [arrays], core_ids=[0])
    return r.results[0]["outT"].transpose(0, 3, 2, 1).reshape(B, N, D)
```

```python
from contextlib import ExitStack

import concourse.bass as bass
from concourse import mybir

ALU = mybir.AluOpType
ACT = mybir.ActivationFunctionType
AX = mybir.AxisListType
F32 = mybir.dt.float32
F32R = mybir.dt.float32r

P = 128
B, N, M, D, E = 16, 112, 375, 512, 256
GROUP = 4
G = B // GROUP
NG = GROUP * N
KD, KE = D // P, E // P
M2 = M + M % 2
MT = -(-M // P)
MROWS = [min(P, M - P * t) for t in range(MT)]
SCORE_SCALE = float(D) ** -0.5
EPS = 1e-6
WARM_UP = 10
DVE_OUT = KD - 1
HALVES = [slice(0, NG // 2), slice(NG // 2, NG)]
ALL = slice(0, NG)


def build(nc: bass.Bass, xT, memT, memN, w_mem, w_memT, w_gateT, vecs, outT):
    with ExitStack() as ctx:
        def sb(name, shape, dt=F32):
            return ctx.enter_context(nc.sbuf_tensor(name, shape, dt))

        def bank(name):
            return ctx.enter_context(nc.psum_tensor(name, [P, 512], F32))

        def sem(name):
            return ctx.enter_context(nc.semaphore(name))

        x = sb("x", [P, G, KD, NG])
        x_hi = sb("x_hi", [P, G, KD, NG], F32R)
        x_lo = sb("x_lo", [P, G, KD, NG], F32R)
        wq = sb("wq", [P, KD, E])
        wq_hi = sb("wq_hi", [P, KD, E], F32R)
        wq_lo = sb("wq_lo", [P, KD, E], F32R)
        wc = sb("wc", [P, KE, D])
        wc_hi = sb("wc_hi", [P, KE, D], F32R)
        wc_lo = sb("wc_lo", [P, KE, D], F32R)
        wg = sb("wg", [P, 2 * KD, D])
        wg_hi = sb("wg_hi", [P, KD, D], F32R)
        wg_lo = sb("wg_lo", [P, KD, D], F32R)
        ww_hi = sb("ww_hi", [P, KE, D], F32R)
        ww_lo = sb("ww_lo", [P, KE, D], F32R)
        bw = sb("bw", [P, 2 * KD])
        half_b = sb("half_b", [P, KD])
        ident = sb("ident", [N, N])
        mean_of = sb("mean_of", [P, P])
        mem_t = sb("mem_t", [P, 2, KE * M2])
        mem_t_hi = sb("mem_t_hi", [P, 2, KE * M2], F32R)
        mem_t_lo = sb("mem_t_lo", [P, 2, KE * M2], F32R)
        mem_n = sb("mem_n", [P, GROUP, MT * E])
        q_hi = sb("q_hi", [P, KE, NG], F32R)
        q_lo = sb("q_lo", [P, KE, NG], F32R)
        neg_max = sb("neg_max", [P, GROUP])
        row_sum = sb("row_sum", [P, GROUP])
        row_inv = sb("row_inv", [P, GROUP])
        probs = sb("probs", [P, GROUP, M])
        aT_hi = sb("aT_hi", [P, 2, KE, NG], F32R)
        aT_lo = sb("aT_lo", [P, 2, KE, NG], F32R)
        spent = wg[:, KD:].rearrange("p k d -> p (k d)")
        gated = spent[:, 0:2 * NG].rearrange("p (s n) -> p s n", s=2)
        squares = spent[:, 2 * NG:4 * NG].rearrange("p (s n) -> p s n", s=2)
        split = wg[:, 0:KD].rearrange("p k d -> p (k d)")
        sq_sum, rstd = split[:, 0:NG], split[:, NG:2 * NG]
        eps = sb("eps", [P, 1])
        probsT = wq[:, :, :].rearrange("p k e -> p (k e)")[:, 0:2 * MT * N].rearrange("p (s n) -> p s n", s=2)
        wg2_hi, wg2_lo = (part[:, 2:].rearrange("p g k n -> p (g k n)")[:, 0:KD * D]
                          .rearrange("p (k d) -> p k d", k=KD) for part in (x_hi, x_lo))

        p_scores = bank("p_scores")
        p_probsT = bank("p_probsT")
        p_aT = bank("p_aT")
        p_q0 = bank("p_q0")
        p_logit = [bank("p_logit0"), bank("p_logit1")]
        p_ctx = [bank("p_ctx0"), bank("p_ctx1")]
        p_q = [p_q0, p_aT]
        p_scores_first = [p_scores, p_ctx[0], p_q0, p_logit[1]]
        p_ww = [p_logit[0], p_ctx[1]]
        p_probsT_first = [p_probsT, p_scores, p_ctx[0], p_q0]
        p_aT_first = [p_aT, p_logit[1]] * (GROUP // 2)
        p_mean_last = [p_scores, p_logit[0]]

        ld_x = {g: sem(f"ld_x_{g}") for g in range(1, G)}
        ld_x0 = [sem(f"ld_x0_{k}") for k in range(KD)]
        ld_wq = [sem(f"ld_wq_{k}") for k in range(KD)]
        ld_wc, ld_wg1, ld_bw = sem("ld_wc"), sem("ld_wg1"), sem("ld_bw")
        ld_wg2 = [sem("ld_wg2_first"), sem("ld_wg2_rest")]
        ld_memT = [sem(f"ld_memT{j}") for j in range(GROUP)]
        ld_memN = [sem(f"ld_memN{j}") for j in range(GROUP)]
        stored = sem("stored")
        mean_of_ok, zeroed, ident_ok, eps_ok, half_b_ok = (
            sem(n) for n in ("mean_of_ok", "zeroed", "ident_ok", "eps_ok", "half_b_ok"))
        x0_hi, x0_lo, x1_hi, xs_hi, x1_lo, xs_lo = (sem(n) for n in ("x0_hi", "x0_lo", "x1_hi", "xs_hi", "x1_lo", "xs_lo"))
        wq_hi_ok, wq_lo_ok = sem("wq_hi_ok"), sem("wq_lo_ok")
        wc_hi_ok, wc_lo_ok = sem("wc_hi_ok"), sem("wc_lo_ok")
        wg_hi_ok, wg_lo_ok = sem("wg_hi_ok"), sem("wg_lo_ok")
        wg2_hi_ok, wg2_lo_ok = sem("wg2_hi_ok"), sem("wg2_lo_ok")
        ww_made, ww_hi_ok, ww_lo_ok = sem("ww_made"), sem("ww_hi_ok"), sem("ww_lo_ok")
        q_made, q_hi_ready, q_ready = sem("q_made"), sem("q_hi_ready"), sem("q_ready")
        memT_hi_ready, memT_ready = sem("memT_hi_ready"), sem("memT_ready")
        scores_made, max_made, exp_made, inv_made, probs_ready = (
            sem(n) for n in ("scores_made", "max_made", "exp_made", "inv_made", "probs_ready"))
        probsT_made, probsT_ready = sem("probsT_made"), sem("probsT_ready")
        aT_made, aT_hi_ready, aT_lo_ready = sem("aT_made"), sem("aT_hi_ready"), sem("aT_lo_ready")
        logit_made, ctx_made, tanh_made, gated_made, fused_made, sq_made = (
            sem(n) for n in ("logit_made", "ctx_made", "tanh_made", "gated_made", "fused_made", "sq_made"))
        sq_added, weighted = sem("sq_added"), sem("weighted")
        sq_sum_made, mean_made, log_made, rstd_made, out_made, pool_out_made = (
            sem(n) for n in ("sq_sum_made", "mean_made", "log_made", "rstd_made", "out_made", "pool_out_made"))

        def f32(ap):
            return ap.bitcast(F32)

        block = ctx.enter_context(nc.Block())

        @block.sync
        def _(sp):
            def load_memT(b, j):
                if not (isinstance(b, int) and b < 2):
                    sp.wait_ge(memT_ready, b - 1)
                sp.dma_start(mem_t[:, j % 2, :], memT[b]).then_inc(ld_memT[j], 16)

            def load_memN(b, j):
                sp.dma_start(mem_n[:, j, :], memN[b]).then_inc(ld_memN[j], 16)

            for k in range(KD):
                sp.dma_start(wq[:, k], w_mem[:, k]).then_inc(ld_wq[k], 16)
                sp.dma_start(x[:, 0, k], xT[0, :, k]).then_inc(ld_x0[k], 16)
            sp.dma_start(wg[:, KD], w_gateT[:, KD]).then_inc(ld_wg2[0], 16)
            for j in range(2):
                load_memT(j, j)
            sp.dma_start(wg[:, KD + 1:], w_gateT[:, KD + 1:]).then_inc(ld_wg2[1], 16)
            sp.dma_start(wg[:, 0:KD], w_gateT[:, 0:KD]).then_inc(ld_wg1, 16)
            for j in range(2, GROUP):
                load_memT(j, j)
            for j in range(GROUP):
                if j == 2:
                    sp.dma_start(x[:, 1], xT[1]).then_inc(ld_x[1], 16)
                load_memN(j, j)
            sp.dma_start(wc[:, :, :], w_memT).then_inc(ld_wc, 16)
            sp.dma_start(bw[:, :], vecs).then_inc(ld_bw, 16)
            for g in range(2, G):
                sp.dma_start(x[:, g], xT[g]).then_inc(ld_x[g], 16)
            with sp.Fori(1, G) as g:
                for j in range(GROUP):
                    sp.wait_ge(aT_made, GROUP * g + (j - GROUP + 1))
                    load_memN(GROUP * g + j, j)
                    load_memT(GROUP * g + j, j)
            with sp.Fori(0, G - 1) as g:
                for c in range(KD):
                    if c == 0:
                        sp.wait_ge(pool_out_made, g + 1)
                    else:
                        sp.wait_ge(out_made, DVE_OUT * g + c)
                    sp.dma_start(outT[g, :, c], x[:, g, c]).then_inc(stored, 16)
            for h, rows in enumerate(HALVES):
                sp.wait_ge(pool_out_made, G + h)
                sp.wait_ge(out_made, DVE_OUT * (G - 1 + h) + 1)
                sp.dma_start(outT[G - 1, :, 0:2, rows], x[:, G - 1, 0:2, rows]).then_inc(stored, 16)
                sp.wait_ge(out_made, DVE_OUT * (G + h))
                sp.dma_start(outT[G - 1, :, 2:, rows], x[:, G - 1, 2:, rows]).then_inc(stored, 16)
            sp.wait_ge(stored, 16 * (KD * (G - 1) + 2 * len(HALVES)))

        @block.tensor
        def _(pe):
            def three(out, w_hi, w_lo, m_hi, m_lo, first, last):
                pe.matmul(out, w_hi, m_hi, start=first, stop=False)
                pe.matmul(out, w_lo, m_hi, start=False, stop=False)
                return pe.matmul(out, w_hi, m_lo, start=False, stop=last)

            def q_part(g, e, k):
                return three(p_q[e][:, 0:NG], wq_hi[:, k, e * P:(e + 1) * P], wq_lo[:, k, e * P:(e + 1) * P],
                             x_hi[:, g, k], x_lo[:, g, k], k == 0, k == KD - 1)

            def product_of_weights(k):
                pe.wait_ge(wg2_lo_ok, k + 1)
                for e in range(KE):
                    mm = three(p_ww[e][:, 0:D], wq_hi[:, k, e * P:(e + 1) * P], wq_lo[:, k, e * P:(e + 1) * P],
                               wg2_hi[:, k], wg2_lo[:, k], k == 0, k == KD - 1)
                    if k == KD - 1:
                        mm.then_inc(ww_made, 1)

            def score(b, j, into=p_scores):
                pe.wait_ge(memT_ready, b + 1)
                for e in range(KE):
                    cols = slice(e * M2, (e + 1) * M2)
                    mm = three(into[0:N, 0:M2], q_hi[:, e, j * N:(j + 1) * N], q_lo[:, e, j * N:(j + 1) * N],
                               mem_t_hi[:, j % 2, cols], mem_t_lo[:, j % 2, cols], e == 0, e == KE - 1)
                mm.then_inc(scores_made, 1)

            def transpose_probs(b, j, into=p_probsT):
                pe.wait_ge(probs_ready, b + 1)
                for t in range(MT):
                    mm = pe.transpose(into[0:MROWS[t], t * N:(t + 1) * N],
                                      probs[0:N, j, t * P:t * P + MROWS[t]], ident[:, :])
                mm.then_inc(probsT_made, 1)

            def attend(b, j, into=p_aT):
                pe.wait_ge(probsT_ready, b + 1)
                pe.wait_ge(ld_memN[j], 16 * (b // GROUP + 1) if isinstance(b, int)
                           else b * (16 // GROUP) + 16 * (GROUP - j) // GROUP)
                for e in range(KE):
                    for t in range(MT):
                        mm = pe.matmul(into[:, e * N:(e + 1) * N],
                                       mem_n[0:MROWS[t], j, t * E + e * P:t * E + (e + 1) * P],
                                       probsT[0:MROWS[t], j % 2, t * N:(t + 1) * N],
                                       start=(t == 0), stop=(t == MT - 1))
                mm.then_inc(aT_made, 1)

            def logits_from_x(g, c, ks=range(KD)):
                for k in ks:
                    three(p_logit[c % 2][:, 0:NG], wg_hi[:, k, c * P:(c + 1) * P],
                          wg_lo[:, k, c * P:(c + 1) * P], x_hi[:, g, k], x_lo[:, g, k], k == 0, False)

            def logits_from_a(g, c, par):
                for e in range(KE):
                    mm = three(p_logit[c % 2][:, 0:NG], ww_hi[:, e, c * P:(c + 1) * P],
                               ww_lo[:, e, c * P:(c + 1) * P], aT_hi[:, par, e], aT_lo[:, par, e],
                               False, e == KE - 1)
                mm.then_inc(logit_made, 1)

            def context(g, c, par, into=None, rows=ALL):
                into = into or p_ctx[c % 2]
                for e in range(KE):
                    mm = three(into[:, rows], wc_hi[:, e, c * P:(c + 1) * P], wc_lo[:, e, c * P:(c + 1) * P],
                               aT_hi[:, par, e, rows], aT_lo[:, par, e, rows], e == 0, e == KE - 1)
                mm.then_inc(ctx_made, 1)

            def mean_square(g):
                pe.wait_ge(sq_sum_made, g + 1)
                pe.matmul(p_scores[:, 0:NG], mean_of[:, :], sq_sum[:, :], start=True, stop=True).then_inc(mean_made, 1)

            pe.wait_ge(mean_of_ok, 1)
            for _ in range(WARM_UP):
                pe.matmul(p_scores[:, 0:P], mean_of[:, :], mean_of[:, :], start=True, stop=True)

            for k in range(KD):
                pe.wait_ge(wq_lo_ok, k + 1)
                pe.wait_ge(x0_lo, k + 1)
                for e in range(KE):
                    mm = q_part(0, e, k)
                    if k == KD - 1:
                        mm.then_inc(q_made, 1)
            product_of_weights(0)
            pe.wait_ge(q_ready, KE)
            score(0, 0, p_scores_first[0])
            score(1, 1, p_scores_first[1])
            product_of_weights(1)
            product_of_weights(2)
            pe.wait_ge(ident_ok, 1)
            transpose_probs(0, 0, p_probsT_first[0])
            product_of_weights(3)
            transpose_probs(1, 1, p_probsT_first[1])
            score(2, 2, p_scores_first[2])
            score(3, 3, p_scores_first[3])
            for j in range(GROUP):
                if j > 1:
                    pe.wait_ge(aT_lo_ready, j - 1)
                attend(j, j, p_aT_first[j])
                if j < 2:
                    pe.wait_ge(ww_lo_ok, 1)
                    for k in (2 * j, 2 * j + 1):
                        pe.wait_ge(wg_lo_ok, k + 1)
                        logits_from_x(0, 0, [k])
                if j == 0:
                    for i in (2, 3):
                        transpose_probs(i, i, p_probsT_first[i])
            pe.wait_ge(ww_lo_ok, KE)

            with pe.Fori(1, G) as g:
                par = (g + 1) % 2
                b = GROUP * g
                pe.wait_ge(xs_lo, g)
                for e in range(KE):
                    if e:
                        pe.wait_ge(aT_lo_ready, b)
                    for k in range(KD):
                        mm = q_part(g, e, k)
                    mm.then_inc(q_made, 1)
                pe.wait_ge(wc_lo_ok, KE)
                logits_from_a(g - 1, 0, par)
                context(g - 1, 0, par)
                pe.wait_ge(q_ready, KE * g + KE)
                score(b, 0)
                logits_from_x(g - 1, 1)
                for j in range(GROUP):
                    if j == GROUP - 1:
                        logits_from_x(g, 0, range(KD // 2))
                    transpose_probs(b + j, j)
                    if j < GROUP - 2:
                        score(b + j + 1, j + 1)
                        attend(b + j, j)
                    if j < GROUP - 1:
                        logits_from_a(g - 1, j + 1, par)
                        if j == GROUP - 2:
                            score(b + j + 1, j + 1)
                        if j:
                            pe.wait_ge(gated_made, KD * g + (j - KD))
                        context(g - 1, j + 1, par)
                    if j < GROUP - 2:
                        pe.wait_ge(tanh_made, KD * g + (j + 1 - KD))
                        logits_from_x(g - 1, j + 2)
                    if j == GROUP - 2:
                        attend(b + j, j)
                        pe.wait_ge(tanh_made, KD * g + (j + 1 - KD))
                    if j == GROUP - 1:
                        logits_from_x(g, 0, range(KD // 2, KD))
                        pe.wait_ge(aT_lo_ready, b + j)
                        attend(b + j, j)
                        mean_square(g - 1)

            par = (G - 1) % 2
            first = KD * (G - 1)
            logits_from_x(G - 1, 1)
            pe.wait_ge(aT_lo_ready, B)
            for c in range(KD):
                logits_from_a(G - 1, c, par)
                if c >= 2:
                    pe.wait_ge(gated_made, first + c - 1)
                if c < KD - 1:
                    context(G - 1, c, par)
                if 1 <= c < KD - 1:
                    pe.wait_ge(tanh_made, first + c)
                    logits_from_x(G - 1, c + 1)
            for h, rows in enumerate(HALVES):
                if h == 1:
                    pe.wait_ge(gated_made, first + KD - 1)
                context(G - 1, KD - 1, par, p_ctx[(KD - 1 + h) % 2], rows)
            pe.wait_ge(sq_added, (KD - 2) * G)
            for h, rows in enumerate(HALVES):
                pe.matmul(p_mean_last[h][:, rows], mean_of[:, :], sq_sum[:, rows], start=True, stop=False)
            for h, rows in enumerate(HALVES):
                pe.wait_ge(sq_made, KD * G + h)
                pe.matmul(p_mean_last[h][:, rows], mean_of[:, :], squares[:, (KD - 1) % 2, rows], start=False, stop=True)\
                    .then_inc(mean_made, 1)

        @block.scalar
        def _(act):
            def exponentials(b, j, scores=p_scores):
                act.wait_ge(max_made, b + 1)
                nc.scalar.activation(probs[0:N, j], scores[0:N, 0:M], ACT.Exp, bias=neg_max[0:N, j:j + 1],
                                     accum_out=row_sum[0:N, j:j + 1]).then_inc(exp_made, 1)

            def read_q(g):
                for e in range(KE):
                    act.wait_ge(q_made, KE * g + e + 1)
                    nc.scalar.activation(q_hi[:, e], p_q[e][:, 0:NG], ACT.Copy, scale=SCORE_SCALE).then_inc(q_hi_ready, 1)

            def high_memory(b, j):
                if isinstance(b, int):
                    if b >= 2:
                        act.wait_ge(scores_made, b - 1)
                    act.wait_ge(ld_memT[j], 16)
                else:
                    act.wait_ge(ld_memT[j], b * (16 // GROUP) + 16 * (GROUP - j) // GROUP)
                nc.scalar.activation(mem_t_hi[:, j % 2], mem_t[:, j % 2], ACT.Copy).then_inc(memT_hi_ready, 1)

            def high_a(b, j, par, bank=p_aT):
                act.wait_ge(aT_made, b + 1)
                nc.scalar.activation(aT_hi[:, par, :, j * N:(j + 1) * N],
                                     bank[:, 0:KE * N].rearrange("p (e n) -> p e n", e=KE),
                                     ACT.Copy).then_inc(aT_hi_ready, 1)

            def tanh(g, c):
                act.wait_ge(logit_made, KD * g + c + 1)
                nc.scalar.activation(gated[:, c % 2], p_logit[c % 2][:, 0:NG], ACT.Tanh, bias=half_b[:, c:c + 1],
                                     scale=0.5).then_inc(tanh_made, 1)

            def square(g, c, h=0, rows=ALL):
                act.wait_ge(fused_made, KD * g + c + h + 1)
                if c >= 2:
                    act.wait_ge(sq_added, (KD - 2) * g + 1)
                nc.scalar.activation(squares[:, c % 2, rows], x[:, g, c, rows], ACT.Square).then_inc(sq_made, 1)

            def weight(g):
                nc.scalar.activation(x[:, g, 0], x[:, g, 0], ACT.Copy, scale=bw[:, KD:KD + 1]).then_inc(weighted, 1)

            def root(count, mean=p_scores, rows=ALL):
                act.wait_ge(mean_made, count)
                nc.scalar.activation(rstd[:, rows], mean[:, rows], ACT.Ln, bias=eps[:, 0:1]).then_inc(log_made, 1)
                act.wait_ge(log_made, count)
                nc.scalar.activation(rstd[:, rows], rstd[:, rows], ACT.Exp, scale=-0.5).then_inc(rstd_made, 1)

            for k in range(KD):
                act.wait_ge(ld_wq[k], 16)
                nc.scalar.activation(wq_hi[:, k], wq[:, k], ACT.Copy).then_inc(wq_hi_ok, 1)
                act.wait_ge(ld_x0[k], 16)
                nc.scalar.activation(x_hi[:, 0, k], x[:, 0, k], ACT.Copy).then_inc(x0_hi, 1)

            def high_wg2(k):
                act.wait_ge(ld_wg2[0 if k == 0 else 1], 16)
                nc.scalar.activation(wg2_hi[:, k], wg[:, KD + k], ACT.Copy).then_inc(wg2_hi_ok, 1)

            high_wg2(0)
            high_memory(0, 0)
            high_memory(1, 1)
            read_q(0)
            for k in range(1, KD):
                high_wg2(k)
            exponentials(0, 0, p_scores_first[0])
            exponentials(1, 1, p_scores_first[1])

            def high_wg(k):
                act.wait_ge(ld_wg1, 16)
                nc.scalar.activation(wg_hi[:, k], wg[:, k], ACT.Copy).then_inc(wg_hi_ok, 1)

            for j in range(2, GROUP):
                high_memory(j, j)
                high_wg(j - 2)
            for e in range(KE):
                act.wait_ge(ww_made, e + 1)
                nc.scalar.activation(ww_hi[:, e], p_ww[e][:, 0:D], ACT.Copy).then_inc(ww_hi_ok, 1)
            for j in range(2, GROUP):
                high_wg(j)
                exponentials(j, j, p_scores_first[j])
            for j in range(GROUP):
                high_a(j, j, 0, p_aT_first[j])
                if j == 0:
                    act.wait_ge(ld_x[1], 16)
                    for k in range(KD):
                        nc.scalar.activation(x_hi[:, 1, k], x[:, 1, k], ACT.Copy).then_inc(x1_hi, 1)
                if j == 2:
                    act.wait_ge(ld_wc, 16)
                    for e in range(KE):
                        nc.scalar.activation(wc_hi[:, e], wc[:, e], ACT.Copy, scale=0.5).then_inc(wc_hi_ok, 1)
            act.wait_ge(half_b_ok, 1)
            act.wait_ge(eps_ok, 1)
            with act.Fori(1, G) as g:
                b = GROUP * g
                high_memory(b, 0)
                read_q(g)
                tanh(g - 1, 0)
                high_memory(b + 1, 1)
                for j in range(GROUP):
                    exponentials(b + j, j)
                    if j == GROUP - 1:
                        tanh(g - 1, j)
                        high_a(b + j - 1, j - 1, g % 2)
                        square(g - 1, j)
                    if 0 < j < GROUP - 1:
                        high_a(b + j - 1, j - 1, g % 2)
                        tanh(g - 1, j)
                    if j < GROUP - 1:
                        square(g - 1, j)
                    if j == 0:
                        weight(g - 1)
                    if j < GROUP - 2:
                        high_memory(b + j + 2, j + 2)
                nc.scalar.preload_act_table_set("natural_log_exp_and_others")
                high_a(b + GROUP - 1, GROUP - 1, g % 2)
                root(g)
            for c in range(KD - 1):
                tanh(G - 1, c)
                square(G - 1, c)
                if c == 0:
                    weight(G - 1)
            tanh(G - 1, KD - 1)
            nc.scalar.preload_act_table_set("natural_log_exp_and_others")
            for h, rows in enumerate(HALVES):
                square(G - 1, KD - 1, h, rows)
            for h, rows in enumerate(HALVES):
                root(G + h, p_mean_last[h], rows)

        @block.vector
        def _(dve):
            def low(out, whole, high, ready, done):
                if ready is not None:
                    dve.wait_ge(*ready)
                nc.vector.tensor_tensor(out, whole, f32(high), ALU.subtract).then_inc(done, 1)

            def neg_row_max(b, j, scores=p_scores):
                dve.wait_ge(scores_made, b + 1)
                nc.vector.tensor_reduce(neg_max[0:N, j:j + 1], scores[0:N, 0:M], AX.X, ALU.max,
                                        negate=True).then_inc(max_made, 1)

            def normalise(b, j):
                dve.wait_ge(exp_made, b + 1)
                nc.vector.reciprocal(row_inv[0:N, j:j + 1], row_sum[0:N, j:j + 1]).then_inc(inv_made, 1)
                dve.wait_ge(inv_made, b + 1)
                nc.vector.tensor_scalar(probs[0:N, j], probs[0:N, j], row_inv[0:N, j:j + 1], None,
                                        ALU.mult).then_inc(probs_ready, 1)

            def read_probsT(b, j, bank=p_probsT):
                dve.wait_ge(probsT_made, b + 1)
                full = (MT - 1) * N
                nc.vector.tensor_copy(probsT[:, j % 2, 0:full], bank[:, 0:full])
                nc.vector.tensor_copy(probsT[0:MROWS[-1], j % 2, full:], bank[0:MROWS[-1], full:MT * N])\
                    .then_inc(probsT_ready, 1)

            def low_q(g):
                for e in range(KE):
                    dve.wait_ge(q_hi_ready, KE * g + e + 1)
                    nc.vector.scalar_tensor_tensor(out=q_lo[:, e], in0=p_q[e][:, 0:NG], scalar=SCORE_SCALE,
                                                   in1=f32(q_hi[:, e]), op0=ALU.mult, op1=ALU.subtract)\
                        .then_inc(q_ready, 1)

            def low_memory(b, j):
                low(mem_t_lo[:, j % 2], mem_t[:, j % 2], mem_t_hi[:, j % 2], (memT_hi_ready, b + 1), memT_ready)

            def low_a(b, j, par, bank=p_aT):
                dve.wait_ge(aT_hi_ready, b + 1)
                low(aT_lo[:, par, :, j * N:(j + 1) * N], bank[:, 0:KE * N].rearrange("p (e n) -> p e n", e=KE),
                    aT_hi[:, par, :, j * N:(j + 1) * N], None, aT_lo_ready)

            def gate_context(g, c, h=0, rows=ALL):
                if not h:
                    dve.wait_ge(tanh_made, KD * g + c + 1)
                dve.wait_ge(ctx_made, KD * g + c + h + 1)
                nc.vector.scalar_tensor_tensor(out=gated[:, c % 2, rows], in0=gated[:, c % 2, rows], scalar=1.0,
                                               in1=p_ctx[(c + h) % 2][:, rows], op0=ALU.add, op1=ALU.mult)\
                    .then_inc(gated_made, 1)

            def fuse(g, c, h=0, rows=ALL):
                dve.wait_ge(gated_made, KD * g + c + h + 1)
                nc.vector.tensor_tensor(x[:, g, c, rows], x[:, g, c, rows], gated[:, c % 2, rows], ALU.add)\
                    .then_inc(fused_made, 1)

            def output(g, c, rows=ALL):
                nc.vector.scalar_tensor_tensor(out=x[:, g, c, rows], in0=x[:, g, c, rows],
                                               scalar=bw[:, KD + c:KD + c + 1], in1=rstd[:, rows],
                                               op0=ALU.mult, op1=ALU.mult).then_inc(out_made, 1)

            nc.vector.memset(mean_of[:, :], 1.0 / D).then_inc(mean_of_ok, 1)
            for k in range(KD):
                low(wq_lo[:, k], wq[:, k], wq_hi[:, k], (wq_hi_ok, k + 1), wq_lo_ok)
                low(x_lo[:, 0, k], x[:, 0, k], x_hi[:, 0, k], (x0_hi, k + 1), x0_lo)

            def low_ww(e):
                low(ww_lo[:, e], p_ww[e][:, 0:D], ww_hi[:, e], (ww_hi_ok, e + 1), ww_lo_ok)

            def low_wg(k):
                low(wg_lo[:, k], wg[:, k], wg_hi[:, k], (wg_hi_ok, k + 1), wg_lo_ok)

            def low_wg2(k):
                low(wg2_lo[:, k], wg[:, KD + k], wg2_hi[:, k], (wg2_hi_ok, k + 1), wg2_lo_ok)

            low_wg2(0)
            low_memory(0, 0)
            low_q(0)
            low_memory(1, 1)
            low_wg2(1)
            neg_row_max(0, 0, p_scores_first[0])
            low_wg2(2)
            neg_row_max(1, 1, p_scores_first[1])
            low_wg2(3)
            normalise(0, 0)
            normalise(1, 1)
            low_memory(2, 2)
            read_probsT(0, 0, p_probsT_first[0])
            low_memory(3, 3)
            read_probsT(1, 1, p_probsT_first[1])
            low_wg(0)
            neg_row_max(2, 2, p_scores_first[2])
            low_ww(0)
            neg_row_max(3, 3, p_scores_first[3])
            low_wg(1)
            normalise(2, 2)
            normalise(3, 3)
            low_wg(2)
            low_wg(3)
            low_ww(1)
            for j in range(GROUP):
                low_a(j, j, 0, p_aT_first[j])
                if j < GROUP - 2:
                    read_probsT(j + 2, j + 2, p_probsT_first[j + 2])
            for e in range(KE):
                dve.wait_ge(wc_hi_ok, e + 1)
                nc.vector.scalar_tensor_tensor(out=wc_lo[:, e], in0=wc[:, e], scalar=0.5, in1=f32(wc_hi[:, e]),
                                               op0=ALU.mult, op1=ALU.subtract).then_inc(wc_lo_ok, 1)
            nc.vector.memset(eps[:, :], EPS).then_inc(eps_ok, 1)
            dve.wait_ge(ld_bw, 16)
            nc.vector.tensor_scalar(half_b[:, :], bw[:, 0:KD], 0.5, None, ALU.mult).then_inc(half_b_ok, 1)
            with dve.Fori(1, G) as g:
                b = GROUP * g
                low_memory(b, 0)
                low_q(g)
                gate_context(g - 1, 0)
                neg_row_max(b, 0)
                low_memory(b + 1, 1)
                for j in range(GROUP):
                    if j < GROUP - 1:
                        normalise(b + j, j)
                    if j == 0:
                        fuse(g - 1, 0)
                    elif j < GROUP - 1:
                        gate_context(g - 1, j)
                        fuse(g - 1, j)
                    read_probsT(b + j, j)
                    if j < GROUP - 1:
                        neg_row_max(b + j + 1, j + 1)
                    if j < GROUP - 2:
                        low_memory(b + j + 2, j + 2)
                    if j == GROUP - 2:
                        normalise(b + j + 1, j + 1)
                        gate_context(g - 1, j + 1)
                        fuse(g - 1, j + 1)
                    low_a(b + j, j, g % 2)
                dve.wait_ge(rstd_made, g)
                for c in range(1, KD):
                    output(g - 1, c)
            for c in range(KD - 1):
                gate_context(G - 1, c)
                fuse(G - 1, c)
            for h, rows in enumerate(HALVES):
                gate_context(G - 1, KD - 1, h, rows)
                fuse(G - 1, KD - 1, h, rows)
            for h, rows in enumerate(HALVES):
                dve.wait_ge(rstd_made, G + h)
                for c in range(1, KD):
                    output(G - 1, c, rows)

        @block.gpsimd
        def _(pool):
            nc.gpsimd.memset(ident[:, :], 0.0).then_inc(zeroed, 1)
            pool.wait_ge(zeroed, 1)
            nc.gpsimd.affine_select(out=ident[:, :], in_=ident[:, :], compare_op=ALU.not_equal, fill=1.0, base=0,
                                    pattern=[[-1, N]], channel_multiplier=1).then_inc(ident_ok, 1)
            for k in range(KD):
                pool.wait_ge(x1_hi, k + 1)
                nc.gpsimd.tensor_tensor(x_lo[:, 1, k], x[:, 1, k], f32(x_hi[:, 1, k]), ALU.subtract)\
                    .then_inc(xs_lo if k == KD - 1 else x1_lo, 1)
            pool.wait_ge(ww_made, KE)

            def split_x(g):
                pool.wait_ge(ld_x[g], 16)
                nc.gpsimd.tensor_copy(x_hi[:, g], x[:, g]).then_inc(xs_hi, 1)
                pool.wait_ge(xs_hi, g - 1)
                nc.gpsimd.tensor_tensor(x_lo[:, g], x[:, g], f32(x_hi[:, g]), ALU.subtract).then_inc(xs_lo, 1)

            split_x(2)

            def add_squares(g, c):
                pool.wait_ge(sq_made, KD * g + c + 1)
                if c == 1:
                    nc.gpsimd.tensor_tensor(sq_sum[:, :], squares[:, 0], squares[:, 1], ALU.add).then_inc(sq_added, 1)
                else:
                    pool.wait_ge(sq_added, (KD - 2) * g + c - 1)
                    nc.gpsimd.tensor_tensor(sq_sum[:, :], sq_sum[:, :], squares[:, c % 2], ALU.add)\
                        .then_inc(sq_added if c < KD - 1 else sq_sum_made, 1)

            def finish(g):
                for c in range(1, KD):
                    add_squares(g, c)
                pool.wait_ge(weighted, g + 1)
                pool.wait_ge(rstd_made, g + 1)
                nc.gpsimd.tensor_tensor(x[:, g, 0], x[:, g, 0], rstd[:, :], ALU.mult).then_inc(pool_out_made, 1)

            finish(0)
            for g in range(3, G):
                split_x(g)
            with pool.Fori(1, G - 1) as g:
                finish(g)
            for c in range(1, KD - 1):
                add_squares(G - 1, c)
            for h, rows in enumerate(HALVES):
                pool.wait_ge(rstd_made, G + h)
                nc.gpsimd.tensor_tensor(x[:, G - 1, 0, rows], x[:, G - 1, 0, rows], rstd[:, rows], ALU.mult)\
                    .then_inc(pool_out_made, 1)


_INS = ["x", "ctx_1024", "L0_xattn_W_mem", "L0_xattn_W_gate", "L0_xattn_b_gate", "L0_xattn_norm_w"]


def kernel(**inputs):
    import numpy as np
    import concourse.bacc as bacc
    from concourse.bass_utils import run_bass_kernel_spmd as run

    x, mem, w_mem, w_gate, b_gate, norm_w = (np.asarray(inputs[n]) for n in _INS)

    def lay(a):
        return np.ascontiguousarray(a)

    padded = np.zeros((B, MT * P, E), mem.dtype)
    padded[:, :M] = mem
    arrays = {
        "xT": lay(x.reshape(G, NG, KD, P).transpose(0, 3, 2, 1)),
        "memT": lay(padded[:, :M2].reshape(B, M2, KE, P).transpose(0, 3, 2, 1)).reshape(B, P, KE * M2),
        "memN": lay(padded.reshape(B, MT, P, E).transpose(0, 2, 1, 3)).reshape(B, P, MT * E),
        "w_mem": lay(w_mem.reshape(KD, P, E).transpose(1, 0, 2)),
        "w_memT": lay(w_mem.reshape(D, KE, P).transpose(2, 1, 0)),
        "w_gateT": lay(w_gate.reshape(D, 2 * KD, P).transpose(2, 1, 0)),
        "vecs": lay(np.concatenate([b_gate.reshape(KD, P), norm_w.reshape(KD, P)]).transpose()),
    }
    nc = bacc.Bacc("TRN2", target_bir_lowering=False, num_devices=1)
    args = [nc.dram_tensor(n, a.shape, mybir.dt.from_np(a.dtype), kind="ExternalInput").ap() for n, a in arrays.items()]
    out = nc.dram_tensor("outT", (G, P, KD, NG), F32, kind="ExternalOutput").ap()
    build(nc, *args, out)
    r = run(nc, [arrays], core_ids=[0])
    return r.results[0]["outT"].transpose(0, 3, 2, 1).reshape(B, N, D)
```
